# Optimizing a Trainium2 kernel written in Bass

```python
import numpy as np
import jax
import jax.numpy as jnp

def _softmax(x, axis=-1):
    return jax.nn.softmax(x, axis=axis)

def _gelu(x):
    return jax.nn.gelu(x, approximate=True)

def _silu(x):
    return jax.nn.silu(x)

def _sigmoid(x):
    return jax.nn.sigmoid(x)

def _layernorm(x, axis=-1, eps=1e-05):
    m = jnp.mean(x, axis=axis, keepdims=True)
    v = jnp.var(x, axis=axis, keepdims=True)
    return (x - m) / jnp.sqrt(v + eps)

def _scatter_add(tgt, idx, src, axis=0):
    return tgt.at[idx].add(src)

def _segment_sum(src, seg, n):
    return jax.ops.segment_sum(src, seg, n)
kernel_name = 'mk_gnn_resnorm_d1_gnn_r8_062f89'

def setup_inputs(seed: int=0):
    np.random.seed(seed)
    _w = jnp.asarray

    def _rec_inputs():
        import jax
        import jax.numpy as jnp
        _gk = jax.random.key(seed)
        x = -0.0003713 + 1 * jax.random.normal(jax.random.fold_in(_gk, 1), (12500, 256), jnp.float32)
        src = jax.random.randint(jax.random.fold_in(_gk, 2), (200000,), 0, 12500, jnp.int32)
        dst = jax.random.randint(jax.random.fold_in(_gk, 3), (200000,), 0, 12500, jnp.int32)
        _o = jnp.argsort(dst, stable=True)
        src = src[_o]
        dst = dst[_o]
        return (x, src, dst)
    x, src, dst = _rec_inputs()

    def _L0_gnn_setup():
        import jax, jax.numpy as jnp
        import numpy as np
        N_NODES = 6250
        N_EDGES = 50000
        D_IN = 256
        EMBED = 256
        HEADS = 8
        HEAD_DIM = EMBED // HEADS

        def mish(x):
            return x * jnp.tanh(jax.nn.softplus(x))
        key = jax.random.key(seed)
        ks = jax.random.split(key, 8)
        nodes = jax.random.normal(ks[0], (N_NODES, D_IN), dtype=jnp.float32)
        senders = jax.random.randint(ks[1], (N_EDGES,), 0, N_NODES, dtype=jnp.int32)
        receivers = jax.random.randint(ks[2], (N_EDGES,), 0, N_NODES, dtype=jnp.int32)
        s = 1.0 / np.sqrt(D_IN)
        Wi = jax.random.normal(ks[3], (D_IN, HEADS, HEAD_DIM), dtype=jnp.float32) * s
        bi = jnp.zeros((HEADS, HEAD_DIM), dtype=jnp.float32)
        Wj = jax.random.normal(ks[4], (D_IN, HEADS, HEAD_DIM), dtype=jnp.float32) * s
        bj = jnp.zeros((HEADS, HEAD_DIM), dtype=jnp.float32)
        a_w = jax.random.normal(ks[5], (HEAD_DIM,), dtype=jnp.float32) / np.sqrt(HEAD_DIM)
        a_b = jnp.zeros((), dtype=jnp.float32)
        return {'nodes': nodes, 'senders': senders, 'receivers': receivers, 'Wi': Wi, 'bi': bi, 'Wj': Wj, 'bj': bj, 'a_w': a_w, 'a_b': a_b}
    _L0_gnn_all = _L0_gnn_setup()
    _L0_gnn_in = {k: v for k, v in _L0_gnn_all.items() if k in ('Wi', 'bi', 'Wj', 'bj', 'a_w', 'a_b')}
    del _L0_gnn_all
    return {'x': x, 'src': src, 'dst': dst, 'L0_gnn_Wi': _L0_gnn_in['Wi'], 'L0_gnn_bi': _L0_gnn_in['bi'], 'L0_gnn_Wj': _L0_gnn_in['Wj'], 'L0_gnn_bj': _L0_gnn_in['bj'], 'L0_gnn_a_w': _L0_gnn_in['a_w'], 'L0_gnn_a_b': _L0_gnn_in['a_b']}

def reference(x, src, dst, L0_gnn_Wi, L0_gnn_bi, L0_gnn_Wj, L0_gnn_bj, L0_gnn_a_w, L0_gnn_a_b):
    import jax
    import jax.numpy as jnp

    def _L0_gnn_ref(nodes, senders, receivers, Wi, bi, Wj, bj, a_w, a_b):
        import jax, jax.numpy as jnp
        import numpy as np
        N_NODES = 6250
        N_EDGES = 50000
        D_IN = 256
        EMBED = 256
        HEADS = 8
        HEAD_DIM = EMBED // HEADS

        def mish(x):
            return x * jnp.tanh(jax.nn.softplus(x))
        n = nodes.shape[0]
        sent = jnp.einsum('ed,dhk->ehk', nodes[senders], Wi) + bi
        recv = jnp.einsum('ed,dhk->ehk', nodes[receivers], Wj) + bj
        x = mish(sent + recv)
        logits = jnp.einsum('ehk,k->eh', x, a_w) + a_b
        maxs = jax.ops.segment_max(logits, receivers, num_segments=n)
        unnorm = jnp.exp(logits - maxs[receivers])
        denom = jax.ops.segment_sum(unnorm, receivers, num_segments=n)
        weights = unnorm / denom[receivers]
        messages = sent * weights[:, :, None]
        out = jax.ops.segment_sum(messages, receivers, num_segments=n)
        return out.reshape(n, -1)
    x = _layernorm(x + _L0_gnn_ref(x, src, dst, L0_gnn_Wi, L0_gnn_bi, L0_gnn_Wj, L0_gnn_bj, L0_gnn_a_w, L0_gnn_a_b), axis=-1)
    return x

_drawn_inputs = setup_inputs


def setup_inputs(seed=0):
    import zlib

    import numpy as np

    out = dict(_drawn_inputs(seed))
    spreads = {'L0_gnn_bi': (0.0, 0.1), 'L0_gnn_bj': (0.0, 0.735)}
    factors = {}
    for name, (base, spread) in spreads.items():
        noise = np.random.default_rng([zlib.crc32(name.encode()), seed]).standard_normal(out[name].shape)
        drawn = base * np.exp(spread * noise) if base else spread * noise
        out[name] = jnp.asarray(drawn.astype(out[name].dtype))
    for name, factor in factors.items():
        out[name] = (out[name] * factor).astype(out[name].dtype)
    return out
```

```python
from contextlib import ExitStack

import concourse.bass as bass
from concourse import mybir

F32 = mybir.dt.float32
F32R = mybir.dt.float32r
I32 = mybir.dt.int32
ALU = mybir.AluOpType
ACT = mybir.ActivationFunctionType

P = 128
D = 256
HEADS = 8
HD = D // HEADS
TILES = 18
GROUP = 3
GROUPS = TILES // GROUP
COLS = GROUP * P
BLOCK_EDGES = TILES * P
FRAME = TILES + 2
ROW = D + HEADS
BATCH = 3
BIG = 1.0e30
STEP = 2.0 ** 90
NO_NODE = 1 << 14
E_MAX = 1.0e9
EPS = 1e-5


class Block_:

    def __init__(self, u, c, blocks):
        self.u, self.c, self.blocks = u, c, blocks
        self.fixed = isinstance(u, int)

    def shift(self, d):
        return Block_(self.u, self.c + d, self.blocks)

    @property
    def exists(self):
        if not self.fixed:
            assert self.c >= -3
            return True
        return 0 <= 3 * self.u + self.c < self.blocks

    @property
    def is_last(self):
        return self.fixed and 3 * self.u + self.c == self.blocks - 1

    @property
    def buf(self):
        return self.c % 3

    @property
    def index(self):
        return self.u * 3 + self.c

    def count(self, per_block, more=0):
        return self.u * (3 * per_block) + (self.c * per_block + more)

    def uses(self, per_use):
        return self.u * per_use + (self.c // 3 + 1) * per_use

    def positive(self, per_block, more=0):
        least = self.u if self.fixed else 1
        return (3 * least + self.c) * per_block + more > 0


def behind(i, g, lag):
    s = g - lag
    return i.shift(s // GROUPS), s % GROUPS


def gnn_program(nc, x, src, dst, wi, bi, wj, bj, aw, ab, out):
    n_nodes, n_edges = x.shape[0], src.shape[0]
    blocks = -(-n_nodes // P)
    last_rows = n_nodes - (blocks - 1) * P
    edge_tiles = -(-n_edges // P)
    bounds = blocks + 1
    assert bounds <= P and edge_tiles <= 2048 and blocks % 2 == 0

    s_dram = nc.dram_tensor("sent_rows", [blocks * P, D], F32).ap()
    r_dram = nc.dram_tensor("received_rows", [blocks * P, 2 * D], F32).ap()
    srcp = nc.dram_tensor("src_padded", [n_edges + BLOCK_EDGES], I32).ap()
    dstp = nc.dram_tensor("dst_padded", [edge_tiles * P + BLOCK_EDGES], I32).ap()
    ptr_dram = nc.dram_tensor("row_starts", [bounds], I32).ap()

    ctx = ExitStack()
    with ctx:
        def sb(name, shape, dt=F32):
            return ctx.enter_context(nc.sbuf_tensor(name, shape, dt))

        def sem(name):
            return ctx.enter_context(nc.semaphore(name))

        ident = sb("ident", [P, P])
        node_col = sb("node_col", [P, P])
        w_sb = sb("w_sb", [P, 2, 2 * D])
        bias = sb("bias", [P, 2 * D])
        aw_sb = sb("aw_sb", [P, 1])
        ab_sb = sb("ab_sb", [P, 1])
        score_w = sb("score_w", [P, BATCH, 2, 32])
        zero_row = sb("zero_row", [1, BLOCK_EDGES], I32)
        none_row = sb("none_row", [1, BLOCK_EDGES + P], I32)
        ones_row = sb("ones_row", [1, P])
        firsts_i = sb("firsts_i", [1, edge_tiles], I32)
        firsts = sb("firsts", [1, edge_tiles])
        bound_i = sb("bound_i", [P, 1], I32)
        bound = sb("bound", [P, 1])
        before = sb("before", [P, edge_tiles])
        n_tiles_before = sb("n_tiles_before", [P, 1])
        at_tile = sb("at_tile", [P, 1])
        at_tile_i = sb("at_tile_i", [P, 1], I32)
        edge_row = sb("edge_row", [P, P], I32)
        before_row = sb("before_row", [P, P])
        n_before = sb("n_before", [P, 1])
        starts_i = sb("starts_i", [P, 1], I32)
        starts = sb("starts", [1, bounds], I32)
        xt = sb("xt", [P, 2, D])
        xT = sb("xT", [P, 2, 2, P])
        sr = sb("sr", [P, 2, 2 * D])
        rhl = sb("rhl", [P, 2, 2, D], F32R)
        src_i = sb("src_i", [P, 3, TILES], I32)
        dst_i = sb("dst_i", [P, 3, TILES], I32)
        s_buf = sb("s_buf", [P, 3, TILES, ROW])
        r_buf = sb("r_buf", [P, 3, 2, D], F32R)
        nbase = sb("nbase", [P, 3])
        dl = sb("dl", [P, 3, TILES])
        dlb = sb("dlb", [P, 3, TILES])
        sel = sb("sel", [P, 3, TILES, P])
        selT = sb("selT", [P, 2, COLS], F32R)
        e_buf = sb("e_buf", [P, 2, 2, COLS])
        h_buf = sb("h_buf", [P, 2, 2, COLS])
        lts = sb("lts", [32 * GROUP, P])
        logit = sb("logit", [P, 3, HEADS, FRAME])
        pen = sb("pen", [P, 3, HEADS * FRAME + 1])
        fwd = sb("fwd", [P, HEADS, FRAME])
        bwd = sb("bwd", [P, HEADS, FRAME])
        dts = sb("dts", [HEADS, 2, P])
        penf = sb("penf", [HEADS, 2, P])
        penb = sb("penb", [HEADS, 2, P])
        tf = sb("tf", [HEADS, P])
        tb = sb("tb", [HEADS, P])
        carry = sb("carry", [HEADS, 2, P])
        top = sb("top", [P, HEADS, TILES])
        diff = sb("diff", [P, HEADS, TILES])
        x_buf = sb("x_buf", [P, 3, D])
        den = sb("den", [P, HEADS])
        rden = sb("rden", [P, HEADS])
        y = sb("y", [P, D])
        yx = sb("yx", [P, D])
        stats = sb("stats", [P, 6])
        mv = sb("mv", [P, 2])
        eps_sb = sb("eps_sb", [P, 1])
        lnv = sb("lnv", [P, 1])
        rs0 = sb("rs0", [P, 1])
        nt = sb("nt", [P, 3])
        rs1 = sb("rs1", [P, 1])
        y_buf = sb("y_buf", [P, 3, D])

        z_ps = ctx.enter_context(nc.psum_tensor("z_ps", [P, 2, 2, 512], F32))
        pm = ctx.enter_context(nc.psum_tensor("pm", [P, 4, 512], F32))
        selT_ps = pm[:, 0, 0:COLS]
        acc_ps = pm[:, 1, 0:ROW]
        lt_ps = pm[0:32 * GROUP, 2, 0:P]
        misc = pm[:, 3, :]
        edge_first_ps = misc[0:HEADS, 0:2 * P]
        ltt_ps = misc[:, 256:256 + 32 * GROUP]
        carry_ps = misc[:, 384:384 + 2 * HEADS]

        def frame_flat(t, k):
            return t[:, k].rearrange("p h f -> p (h f)")

        s_const = sem("s_const")
        s_pad = sem("s_pad")
        s_first = sem("s_first")
        s_fill = sem("s_fill")
        s_pool_const = sem("s_pool_const")
        s_dve_const = sem("s_dve_const")
        s_firsts_f = sem("s_firsts_f")
        s_bc = sem("s_bc")
        s_at = sem("s_at")
        s_edge_row = sem("s_edge_row")
        s_starts_i = sem("s_starts_i")
        s_starts_d = sem("s_starts_d")
        s_starts = sem("s_starts")
        s_setup = sem("s_setup")
        s_xt = [sem(f"s_xt{a}") for a in range(2)]
        s_xtr = sem("s_xtr")
        s_xT = sem("s_xT")
        s_proj = sem("s_proj")
        s_sr = sem("s_sr")
        s_rhi = sem("s_rhi")
        s_rlo = sem("s_rlo")
        s_s_out = [sem(f"s_s_out{a}") for a in range(2)]
        s_r_out = [sem(f"s_r_out{a}") for a in range(2)]

        src_in = [sem(f"src_in{k}") for k in range(3)]
        dst_in = [sem(f"dst_in{k}") for k in range(3)]
        r_in = [sem(f"r_in{k}") for k in range(3)]
        x_in = [sem(f"x_in{k}") for k in range(3)]
        gathered = [[sem(f"gathered{k}_{g}") for g in range(GROUPS)] for k in range(3)]
        y_out = sem("y_out")
        y_free = sem("y_free")
        prepped = sem("prepped")
        prep_step = sem("prep_step")
        sel_done = sem("sel_done")
        selT_tr = sem("selT_tr")
        selT_done = sem("selT_done")
        z_done = sem("z_done")
        exp_done = sem("exp_done")
        cut_done = sem("cut_done")
        sq_done = sem("sq_done")
        ln_done = sem("ln_done")
        r_done = sem("r_done")
        h_done = sem("h_done")
        score_done = sem("score_done")
        lt_done = sem("lt_done")
        ltt_done = sem("ltt_done")
        logit_done = sem("logit_done")
        ends_tr = sem("ends_tr")
        ends_done = sem("ends_done")
        pens_done = sem("pens_done")
        scan_done = sem("scan_done")
        scan_tr = sem("scan_tr")
        tscan_done = sem("tscan_done")
        carry_done = sem("carry_done")
        carry_tr = sem("carry_tr")
        carry_in = sem("carry_in")
        rescan_done = sem("rescan_done")
        top_done = sem("top_done")
        diff_done = sem("diff_done")
        p_done = sem("p_done")
        msg_done = sem("msg_done")
        out_done = sem("out_done")
        den_done = sem("den_done")
        rden_done = sem("rden_done")
        acc_read = sem("acc_read")
        yx_done = sem("yx_done")
        stats_done = sem("stats_done")
        mv_done = sem("mv_done")
        lnv_done = sem("lnv_done")
        rs0_done = sem("rs0_done")
        newton = sem("newton")
        y_done = sem("y_done")
        sp_passed = sem("sp_passed")
        pool_passed = sem("pool_passed")
        dve_passed = sem("dve_passed")

        block = ctx.enter_context(nc.Block())

        def iterations(eng, body, first=-1, last=None):
            last = blocks + 3 if last is None else last
            turns = (blocks - 2) // 3
            for c in range(first, min(3, last + 1)):
                body(Block_(0, c, blocks))
            if turns > 1:
                with eng.Fori(1, turns) as u:
                    for c in range(3):
                        body(Block_(u, c, blocks))
            for c in range(3 * max(turns, 1), last + 1):
                body(Block_(0, c, blocks))

        @block.sync
        def _(sp):
            sp.dma_start(firsts_i[0:1, :], dst.rearrange("(a e) -> a e", a=1)[:, 0:n_edges:P],
                         allow_slow_non_contiguous=True).then_inc(s_first, 16)
            for k in range(2):
                sp.dma_start(w_sb[:, k, 0:D], wi[k * P:(k + 1) * P, :]).then_inc(s_const, 16)
                sp.dma_start(w_sb[:, k, D:2 * D], wj[k * P:(k + 1) * P, :]).then_inc(s_const, 16)
            sp.dma_start(bias[:, 0:D], bi.broadcast_to([P, D])).then_inc(s_const, 16)
            sp.dma_start(bias[:, D:2 * D], bj.broadcast_to([P, D])).then_inc(s_const, 16)
            for g in range(P // HD):
                sp.dma_start(aw_sb[g * HD:(g + 1) * HD, :], aw).then_inc(s_const, 16)
            sp.dma_start(ab_sb[:, :], ab.broadcast_to([P, 1])).then_inc(s_const, 16)
            sp.dma_start(srcp[0:n_edges], src).then_inc(s_pad, 16)
            sp.dma_start(dstp[0:n_edges], dst).then_inc(s_pad, 16)
            sp.wait_ge(s_fill, 2)
            sp.dma_start(srcp[n_edges:n_edges + BLOCK_EDGES].rearrange("(a e) -> a e", a=1),
                         zero_row[:, :]).then_inc(s_pad, 16)
            tail = edge_tiles * P + BLOCK_EDGES - n_edges
            sp.dma_start(dstp[n_edges:n_edges + tail].rearrange("(a e) -> a e", a=1),
                         none_row[:, 0:tail]).then_inc(s_pad, 16)

            def project(v, a, rows=P, warm=True):
                if warm:
                    sp.wait_ge(s_xtr, v * 2 + (a - 1))
                    sp.sem_inc(sp_passed, 1)
                base = v * (2 * P) + a * P
                sp.dma_start(xt[0:rows, a, :], x[bass.ds(base, rows), :]).then_inc(s_xt[a], 16)
                if warm:
                    sp.wait_ge(s_rlo, v * 2 + (a - 1))
                    sp.sem_inc(sp_passed, 1)
                    store_r(v * (2 * P) + (a - 2) * P, a)

            def store_r(base, a):
                sp.dma_start(r_dram[bass.ds(base, P), :],
                             rhl[:, a].bitcast(F32).rearrange("p a b -> p (a b)")).then_inc(s_r_out[a], 16)

            half = blocks // 2
            for a in range(2):
                project(0, a, warm=False)
            if half > 2:
                with sp.Fori(1, half - 1) as v:
                    for a in range(2):
                        project(v, a)
            project(half - 1, 0)
            project(half - 1, 1, rows=last_rows)
            for a in range(2):
                sp.wait_ge(s_rlo, blocks - 1 + a)
                store_r((blocks - 2 + a) * P, a)

            sp.wait_ge(s_starts_i, 1)
            sp.dma_start(ptr_dram.rearrange("(b a) -> b a", a=1), starts_i[0:bounds, :]).then_inc(s_starts_d, 16)
            sp.wait_ge(s_starts_d, 16)
            sp.dma_start(starts[0:1, :], ptr_dram.rearrange("(a b) -> a b", a=1)).then_inc(s_starts, 16)
            sp.wait_ge(s_starts, 16)
            sp.wait_ge(s_pad, 64)
            for a in range(2):
                sp.wait_ge(s_r_out[a], 16 * half)
            sp.sem_inc(y_free, 3)

            def load(j):
                old = j.shift(-3)
                start = sp.value_load(starts[0:1, bass.ds(j.index, 1)], min_val=0, max_val=n_edges)
                first_row = j.count(P)
                if old.exists:
                    for g in range(GROUPS):
                        sp.wait_ge(gathered[old.buf][g], old.uses(16 * GROUP))
                    sp.sem_inc(sp_passed, 1)
                    sp.wait_ge(prepped, old.count(1, 1))
                    sp.sem_inc(sp_passed, 1)
                    sp.wait_ge(z_done, old.count(GROUPS, GROUPS))
                    sp.sem_inc(sp_passed, 1)
                k = j.buf
                sp.dma_start(src_i[:, k, :], srcp[bass.ds(start, BLOCK_EDGES)].rearrange(
                    "(p j) -> p j", j=TILES)).then_inc(src_in[k], 16)
                sp.dma_start(dst_i[:, k, :], dstp[bass.ds(start, BLOCK_EDGES)].rearrange(
                    "(p j) -> p j", j=TILES)).then_inc(dst_in[k], 16)
                sp.dma_start(r_buf[:, k].bitcast(F32).rearrange("p a b -> p (a b)"),
                             r_dram[bass.ds(first_row, P), :]).then_inc(r_in[k], 16)

            def load_x(i):
                old, k = i.shift(-3), i.buf
                rows = last_rows if i.is_last else P
                first_row = i.count(P)
                if old.exists:
                    sp.wait_ge(yx_done, old.count(1, 1))
                    sp.sem_inc(sp_passed, 1)
                sp.dma_start(x_buf[0:rows, k, :], x[bass.ds(first_row, rows), :]).then_inc(x_in[k], 16)

            def store_y(b):
                rows = last_rows if b.is_last else P
                first_row = b.count(P)
                sp.wait_ge(y_done, b.count(1, 1))
                sp.sem_inc(sp_passed, 1)
                sp.dma_start(out[bass.ds(first_row, rows), :], y_buf[0:rows, b.buf, :]).then_inc(y_out, 16)
                sp.wait_ge(y_out, b.count(16, 16))
                sp.sem_inc(y_free, 1)

            load(Block_(0, 0, blocks))

            def body(i):
                if i.shift(2).exists:
                    load(i.shift(2))
                if i.exists:
                    load_x(i)
                if i.shift(-3).exists:
                    store_y(i.shift(-3))

            iterations(sp, body)

        @block.gpsimd
        def _(pool):
            pool.memset(zero_row[:, :], 0).then_inc(s_fill, 1)
            pool.memset(none_row[:, :], NO_NODE).then_inc(s_fill, 1)
            pool.memset(ones_row[:, :], 1.0).then_inc(s_pool_const, 1)
            pool.memset(ident[:, :], 0.0).then_inc(s_pool_const, 1)
            pool.iota(node_col[:, :], pattern=[[1, P]], base=0, channel_multiplier=0,
                      allow_small_or_imprecise_dtypes=True).then_inc(s_pool_const, 1)
            pool.iota(bound_i[:, :], pattern=[[0, 1]], base=0, channel_multiplier=P).then_inc(s_pool_const, 1)
            pool.wait_ge(s_pool_const, 4)
            pool.affine_select(out=ident[:, :], in_=ident[:, :], compare_op=ALU.not_equal, fill=1.0,
                               base=0, pattern=[[-1, P]], channel_multiplier=1).then_inc(s_pool_const, 1)
            pool.wait_ge(s_pad, 64)
            pool.wait_ge(s_at, 1)
            pool.indirect_dma_start(
                out=edge_row[0:bounds, :], out_offset=None,
                in_=dstp[0:edge_tiles * P].rearrange("(t e) -> t e", e=P),
                in_offset=bass.IndirectOffsetOnAxis(ap=at_tile_i[0:bounds, 0:1], axis=0),
            ).then_inc(s_edge_row, 16)

            def store_s(v, a):
                pool.wait_ge(s_sr, v * 2 + (a + 1))
                pool.dma_start(s_dram[bass.ds(v * (2 * P) + a * P, P), :],
                               sr[:, a, 0:D]).then_inc(s_s_out[a], 16)

            for a in range(2):
                store_s(0, a)
            with pool.Fori(1, blocks // 2) as v:
                for a in range(2):
                    store_s(v, a)
            for a in range(2):
                pool.wait_ge(s_s_out[a], 16 * (blocks // 2))

            def body(j):
                k, old = j.buf, j.shift(-3)
                pool.wait_ge(src_in[k], j.uses(16))
                pool.sem_inc(pool_passed, 1)
                for g in range(GROUPS):
                    if old.exists:
                        pool.wait_ge(out_done, old.count(GROUPS, g + 1))
                        pool.sem_inc(pool_passed, 1)
                    for t in range(GROUP * g, GROUP * (g + 1)):
                        pool.indirect_dma_start(
                            out=s_buf[:, k, t, 0:D], out_offset=None, in_=s_dram,
                            in_offset=bass.IndirectOffsetOnAxis(ap=src_i[:, k, t:t + 1], axis=0),
                        ).then_inc(gathered[k][g], 16)

            iterations(pool, body, first=0, last=blocks - 1)

        @block.scalar
        def _(act):
            act.preload_act_table_set("natural_log_exp_and_others")

            def project(v, a, warm):
                act.wait_ge(s_xtr, v * 2 + (a + 1))
                if warm:
                    act.wait_ge(s_proj, v * 2 + (a - 1))
                act.activation(xT[:, a].rearrange("p k n -> p (k n)"), z_ps[:, a, 0, 0:2 * P],
                               ACT.Copy).then_inc(s_xT, 1)
                act.wait_ge(s_sr, v * 2 + (a + 1))
                if warm:
                    act.wait_ge(s_r_out[a], v * 16)
                act.activation(rhl[:, a, 0, :], sr[:, a, D:2 * D], ACT.Copy).then_inc(s_rhi, 1)

            for a in range(2):
                project(0, a, False)
            with act.Fori(1, blocks // 2) as v:
                for a in range(2):
                    project(v, a, True)

            def slot(i, g):
                par = g % 2
                b = i.shift(-1)
                if g == GROUPS - 1 and b.exists:
                    act.wait_ge(diff_done, b.count(1, 1))
                    act.activation(s_buf[:, b.buf, :, D:ROW].rearrange("p j h -> p h j"), diff[:, :, :],
                                   ACT.Exp).then_inc(p_done, 1)
                j, h = behind(i, g, 2)
                if j.exists and h % BATCH == BATCH - 1:
                    w = h // BATCH
                    act.wait_ge(score_done, j.count(GROUPS, h + 1))
                    if j.positive(2, w):
                        act.wait_ge(ltt_done, j.count(2, w))
                    act.activation(lts[:, :], lt_ps, ACT.Copy).then_inc(lt_done, 1)
                if i.exists:
                    act.wait_ge(z_done, i.count(GROUPS, g + 1))
                    act.activation(e_buf[:, par], z_ps[:, par, :, 0:COLS], ACT.Exp).then_inc(exp_done, 1)
                j, h = behind(i, g, -2)
                if j.exists:
                    act.wait_ge(selT_tr, j.count(GROUPS, h + 1))
                    act.activation(selT[:, par, :], selT_ps, ACT.Copy).then_inc(selT_done, 1)
                if i.exists:
                    act.wait_ge(cut_done, i.count(GROUPS, g + 1))
                    act.activation(e_buf[:, par], e_buf[:, par], ACT.Square, bias=1.0).then_inc(sq_done, 1)
                    act.wait_ge(sq_done, i.count(GROUPS, g + 1))
                    act.activation(e_buf[:, par], e_buf[:, par], ACT.Ln, bias=1.0).then_inc(ln_done, 1)
                    act.wait_ge(ln_done, i.count(GROUPS, g + 1))
                    act.activation(e_buf[:, par], e_buf[:, par], ACT.Exp, scale=-1.0).then_inc(r_done, 1)
                b = i.shift(-3)
                if g == 1 and b.exists:
                    act.wait_ge(mv_done, b.count(1, 1))
                    act.activation(lnv[:, :], mv[:, 1:2], ACT.Ln, bias=eps_sb[:, 0:1]).then_inc(lnv_done, 1)
                    act.wait_ge(lnv_done, b.count(1, 1))
                    act.activation(rs0[:, :], lnv[:, :], ACT.Exp, scale=-0.5).then_inc(rs0_done, 1)

            def body(i):
                for g in range(GROUPS):
                    slot(i, g)

            iterations(act, body)

        @block.tensor
        def _(pe):
            pe.wait_ge(s_pool_const, 5)
            pe.wait_ge(s_firsts_f, 1)
            for c in range(0, edge_tiles, 512):
                m = min(512, edge_tiles - c)
                last = pe.matmul(pm[:, c // 512, 0:m], ones_row[0:1, :], firsts[0:1, c:c + m],
                                 start=True, stop=True)
            last.then_inc(s_bc, 1)

            def transpose_x(v, a, warm):
                pe.wait_ge(s_xt[a], v * 16 + 16)
                if warm:
                    pe.wait_ge(s_xT, v * 2 + (a - 1))
                for k in range(2):
                    last = pe.transpose(z_ps[:, a, 0, k * P:(k + 1) * P], xt[:, a, k * P:(k + 1) * P], ident[:, :])
                last.then_inc(s_xtr, 1)

            def product(t2, a, warm):
                pe.wait_ge(s_xT, t2 + (a + 1))
                if warm:
                    pe.wait_ge(s_sr, t2 + (a - 1))
                for k in range(2):
                    last = pe.matmul(z_ps[:, a, 1, :], xT[:, a, k, :], w_sb[:, k, :], start=k == 0, stop=k == 1)
                last.then_inc(s_proj, 1)

            pe.wait_ge(s_const, 16 * (7 + P // HD))
            transpose_x(0, 0, False)
            transpose_x(0, 1, False)
            product(0, 0, False)
            transpose_x(1, 0, True)
            product(0, 1, False)
            transpose_x(1, 1, True)
            product(2, 0, True)
            with pe.Fori(2, blocks // 2) as v:
                transpose_x(v, 0, True)
                product(v * 2 - 2, 1, True)
                transpose_x(v, 1, True)
                product(v * 2, 0, True)
            product(blocks - 2, 1, True)
            pe.wait_ge(s_setup, 1)
            pe.wait_ge(s_sr, blocks)

            def slot(i, g):
                par = g % 2
                if i.exists:
                    k = i.buf
                    pe.wait_ge(selT_done, i.count(GROUPS, g + 1))
                    if g == 0:
                        pe.wait_ge(r_in[k], i.uses(16))
                    if i.positive(GROUPS, g - 1):
                        pe.wait_ge(h_done, i.count(GROUPS, g - 1))
                    pe.wait_ge(gathered[k][g], i.uses(16 * GROUP))
                    for hf in range(2):
                        f = slice(hf * P, (hf + 1) * P)
                        for part in range(2):
                            pe.matmul(z_ps[:, par, hf, 0:COLS], r_buf[:, k, part, f], selT[:, par, :],
                                      start=part == 0, stop=False)
                        for t in range(GROUP):
                            last = pe.matmul(z_ps[:, par, hf, t * P:(t + 1) * P], s_buf[:, k, GROUP * g + t, f],
                                             ident[:, :], start=False, stop=t == GROUP - 1)
                    last.then_inc(z_done, 1)
                j, h = behind(i, g, -2)
                if j.exists:
                    pe.wait_ge(sel_done, j.count(GROUPS, h + 1))
                    if j.positive(GROUPS, h):
                        pe.wait_ge(selT_done, j.count(GROUPS, h))
                    for t in range(GROUP):
                        last = pe.transpose(selT_ps[:, t * P:(t + 1) * P], sel[:, j.buf, GROUP * h + t, :], ident[:, :])
                    last.then_inc(selT_tr, 1)
                j, h = behind(i, g, 1)
                if j.exists:
                    w, v = h // BATCH, h % BATCH
                    pe.wait_ge(h_done, j.count(GROUPS, h + 1))
                    if v == 0 and j.positive(2, w):
                        pe.wait_ge(lt_done, j.count(2, w))
                    for hf in range(2):
                        for t in range(GROUP):
                            last = pe.matmul(lt_ps[32 * t:32 * t + 32, :], score_w[:, v, hf, :],
                                             h_buf[:, 1 - par, hf, t * P:(t + 1) * P],
                                             start=v == 0 and hf == 0, stop=v == BATCH - 1 and hf == 1,
                                             tile_position=(0, 32 * t))
                    last.then_inc(score_done, 1)
                j, h = behind(i, g, 3)
                if j.exists and h % BATCH == BATCH - 1:
                    w = h // BATCH
                    pe.wait_ge(lt_done, j.count(2, w + 1))
                    if w == 1:
                        pe.wait_ge(ends_done, j.count(1, 1))
                    elif j.positive(1):
                        pe.wait_ge(carry_in, j.count(1))
                    pe.transpose(ltt_ps, lts[:, :], ident[0:32 * GROUP, 0:32 * GROUP]).then_inc(ltt_done, 1)
                b = i.shift(-1)
                if b.exists and g == 0:
                    pe.wait_ge(prepped, b.count(1, 1))
                    pe.wait_ge(logit_done, b.count(2, 1))
                    for n, j_ in enumerate((0, TILES - 1)):
                        last = pe.matmul(edge_first_ps[:, n * P:(n + 1) * P],
                                         dlb[:, b.buf, j_:j_ + 1].broadcast_to([P, HEADS]), ident[:, :],
                                         start=True, stop=True)
                    last.then_inc(ends_tr, 1)
                if b.exists and g == 3:
                    pe.wait_ge(scan_done, b.count(1, 1))
                    pe.matmul(edge_first_ps[:, 0:P], fwd[:, :, TILES], ident[:, :], start=True, stop=True)
                    pe.matmul(edge_first_ps[:, P:2 * P], bwd[:, :, 1], ident[:, :],
                              start=True, stop=True).then_inc(scan_tr, 1)
                if b.exists and g == 4:
                    pe.wait_ge(carry_done, b.count(1, 1))
                    for n in range(2):
                        last = pe.matmul(carry_ps[:, n * HEADS:(n + 1) * HEADS], carry[:, n, :],
                                         ident[0:HEADS, 0:HEADS], start=True, stop=True)
                    last.then_inc(carry_tr, 1)
                j, h = behind(i, g, 12)
                if j.exists:
                    pe.wait_ge(msg_done, j.count(GROUPS, h + 1))
                    if h == 0 and j.positive(1):
                        pe.wait_ge(acc_read, j.count(1))
                    for t in range(GROUP * h, GROUP * (h + 1)):
                        last = pe.matmul(acc_ps, sel[:, j.buf, t, :], s_buf[:, j.buf, t, :],
                                         start=t == 0, stop=t == TILES - 1)
                    last.then_inc(out_done, 1)

            def body(i):
                for g in range(GROUPS):
                    slot(i, g)

            iterations(pe, body)

        @block.vector
        def _(dve):
            dve.memset(score_w[:, :, :, :], 0.0).then_inc(s_dve_const, 1)
            dve.memset(pen[:, :, :], 0.0).then_inc(s_dve_const, 1)
            dve.memset(eps_sb[:, :], EPS).then_inc(s_dve_const, 1)
            dve.memset(carry[:, :, :], -BIG).then_inc(s_dve_const, 1)
            dve.memset(penf[:, :, :], 0.0).then_inc(s_dve_const, 1)
            dve.memset(penb[:, :, :], 0.0).then_inc(s_dve_const, 1)
            for k in range(3):
                dve.memset(nbase[:, k:k + 1], -float(P * k)).then_inc(s_dve_const, 1)
            dve.wait_ge(s_dve_const, 9)
            for k in range(3):
                last = dve.memset(pen[:, k, 0:HEADS * FRAME + 1:FRAME], -BIG)
            last.then_inc(s_dve_const, 1)

            dve.wait_ge(s_first, 16)
            dve.tensor_copy(firsts[0:1, :], firsts_i[0:1, :]).then_inc(s_firsts_f, 1)
            dve.wait_ge(s_pool_const, 5)
            dve.tensor_copy(bound[:, :], bound_i[:, :]).then_inc(s_firsts_f, 1)
            dve.wait_ge(s_bc, 1)
            dve.wait_ge(s_firsts_f, 2)
            dve.tensor_scalar(before[:, :], pm[:, :, :].rearrange("p a b -> p (a b)")[:, 0:edge_tiles],
                              bound[:, 0:1], None, ALU.is_lt).then_inc(s_firsts_f, 1)
            dve.wait_ge(s_firsts_f, 3)
            dve.reduce_sum(n_tiles_before[:, :], before[:, :], mybir.AxisListType.X).then_inc(s_firsts_f, 1)
            dve.wait_ge(s_firsts_f, 4)
            dve.tensor_scalar(at_tile[:, :], n_tiles_before[:, :], -1.0, 0.0, ALU.add, ALU.max).then_inc(s_firsts_f, 1)
            dve.wait_ge(s_firsts_f, 5)
            dve.tensor_copy(at_tile_i[:, :], at_tile[:, :]).then_inc(s_at, 1)

            dve.wait_ge(s_const, 16 * (7 + P // HD))

            def project(v, a, warm):
                dve.wait_ge(s_proj, v * 2 + (a + 1))
                if warm:
                    dve.wait_ge(s_s_out[a], v * 16)
                dve.tensor_tensor(sr[:, a, :], z_ps[:, a, 1, :], bias[:, :], ALU.add).then_inc(s_sr, 1)
                dve.wait_ge(s_rhi, v * 2 + (a + 1))
                dve.tensor_tensor(rhl[:, a, 1, :], sr[:, a, D:2 * D], rhl[:, a, 0, :].bitcast(F32),
                                  ALU.subtract).then_inc(s_rlo, 1)

            for a in range(2):
                project(0, a, False)
            with dve.Fori(1, blocks // 2) as v:
                for a in range(2):
                    project(v, a, True)

            dve.wait_ge(s_edge_row, 16)
            dve.tensor_scalar(before_row[0:bounds, :], edge_row[0:bounds, :], bound[0:bounds, 0:1], None,
                              ALU.is_lt).then_inc(s_firsts_f, 1)
            dve.wait_ge(s_firsts_f, 6)
            dve.reduce_sum(n_before[0:bounds, :], before_row[0:bounds, :], mybir.AxisListType.X).then_inc(s_firsts_f, 1)
            dve.wait_ge(s_firsts_f, 7)
            dve.scalar_tensor_tensor(starts_i[0:bounds, :], at_tile[0:bounds, :], float(P), n_before[0:bounds, :],
                                     ALU.mult, ALU.add).then_inc(s_starts_i, 1)
            for hf in range(2):
                for q in range(P // HD):
                    for v in range(BATCH):
                        at = v * HEADS + hf * (P // HD) + q
                        last = dve.tensor_scalar(score_w[q * HD:(q + 1) * HD, v, hf, at:at + 1],
                                                 aw_sb[q * HD:(q + 1) * HD, :], -2.0, None, ALU.mult)
            last.then_inc(s_setup, 1)

            def prep(j):
                k = j.buf
                dve.wait_ge(dst_in[k], j.uses(16))
                dve.tensor_scalar(dl[:, k, :], dst_i[:, k, :], nbase[:, k:k + 1], None, ALU.add).then_inc(prep_step, 1)
                dve.memset(logit[:, k, :, 0:FRAME:FRAME - 1], -BIG)
                dve.wait_ge(prep_step, j.count(3, 1))
                dve.tensor_scalar(dlb[:, k, :], dl[:, k, :], STEP, None, ALU.mult).then_inc(prep_step, 1)
                dve.tensor_scalar(nbase[:, k:k + 1], nbase[:, k:k + 1], -3.0 * P, None, ALU.add).then_inc(prep_step, 1)
                dve.wait_ge(prep_step, j.count(3, 3))
                dve.tensor_tensor(
                    pen[:, k, 0:HEADS * FRAME].rearrange("p (h f) -> p h f", f=FRAME)[:, :, 2:TILES + 1],
                    dlb[:, k, None, 0:TILES - 1].broadcast_to([P, HEADS, TILES - 1]),
                    dlb[:, k, None, 1:TILES].broadcast_to([P, HEADS, TILES - 1]), ALU.subtract).then_inc(prepped, 1)

            def scans(k):
                dve.tensor_tensor_scan(fwd[:, :, :].rearrange("p h f -> p (h f)"), pen[:, k, 0:HEADS * FRAME],
                                       frame_flat(logit, k), -BIG, ALU.add, ALU.max)
                return dve.tensor_tensor_scan(bwd[:, :, :].rearrange("p h f -> p (h f)")[:, ::-1],
                                              pen[:, k, 1:HEADS * FRAME + 1][:, ::-1],
                                              frame_flat(logit, k)[:, ::-1], -BIG, ALU.add, ALU.max)

            def finish_a(b):
                k = b.buf
                dve.wait_ge(out_done, b.count(GROUPS, GROUPS))
                dve.tensor_scalar(den[:, :], acc_ps[:, D:ROW], 1e-30, None, ALU.max).then_inc(den_done, 1)
                dve.wait_ge(den_done, b.count(1, 1))
                dve.reciprocal(rden[:, :], den[:, :]).then_inc(rden_done, 1)
                dve.wait_ge(rden_done, b.count(1, 1))
                dve.tensor_tensor(y[:, :].rearrange("p (h c) -> p h c", h=HEADS),
                                  acc_ps[:, 0:D].rearrange("p (h c) -> p h c", h=HEADS),
                                  rden[:, :, None].broadcast_to([P, HEADS, HD]), ALU.mult).then_inc(acc_read, 1)
                dve.wait_ge(acc_read, b.count(1, 1))
                dve.wait_ge(x_in[k], b.uses(16))
                dve.tensor_tensor(yx[:, :], y[:, :], x_buf[:, k, :], ALU.add).then_inc(yx_done, 1)
                dve.wait_ge(yx_done, b.count(1, 1))
                dve.bn_stats(stats[:, :], yx[:, :]).then_inc(stats_done, 1)
                dve.wait_ge(stats_done, b.count(1, 1))
                dve.sem_inc(dve_passed, 1)
                dve.bn_aggr(mv[:, :], stats[:, :]).then_inc(mv_done, 1)

            def finish_b(b):
                dve.wait_ge(rs0_done, b.count(1, 1))
                dve.scalar_tensor_tensor(nt[:, 0:1], mv[:, 1:2], EPS, rs0[:, :], ALU.add, ALU.mult).then_inc(newton, 1)
                dve.wait_ge(newton, b.count(4, 1))
                dve.tensor_tensor(nt[:, 1:2], nt[:, 0:1], rs0[:, :], ALU.mult).then_inc(newton, 1)
                dve.wait_ge(newton, b.count(4, 2))
                dve.tensor_scalar(nt[:, 2:3], nt[:, 1:2], -0.5, 1.5, ALU.mult, ALU.add).then_inc(newton, 1)
                dve.wait_ge(newton, b.count(4, 3))
                dve.tensor_tensor(rs1[:, :], nt[:, 2:3], rs0[:, :], ALU.mult).then_inc(newton, 1)
                dve.wait_ge(newton, b.count(4, 4))
                dve.wait_ge(y_free, b.count(1, 1))
                dve.tensor_scalar(y_buf[:, b.buf, :], yx[:, :], mv[:, 0:1], rs1[:, 0:1], ALU.subtract,
                                  ALU.mult).then_inc(y_done, 1)

            def slot(i, g):
                par = g % 2
                if i.exists:
                    dve.wait_ge(exp_done, i.count(GROUPS, g + 1))
                    dve.tensor_scalar(e_buf[:, par], e_buf[:, par], E_MAX, None, ALU.min).then_inc(cut_done, 1)
                if g == 0 and i.shift(1).exists:
                    prep(i.shift(1))
                j, h = behind(i, g, -5)
                if j.exists:
                    old = j.shift(-3)
                    dve.wait_ge(prepped, j.count(1, 1))
                    if old.exists:
                        dve.wait_ge(out_done, old.count(GROUPS, h + 1))
                    dve.tensor_tensor(
                        sel[:, j.buf, GROUP * h:GROUP * (h + 1), :],
                        node_col[:, None, :].broadcast_to([P, GROUP, P]),
                        dl[:, j.buf, GROUP * h:GROUP * (h + 1), None].broadcast_to([P, GROUP, P]),
                        ALU.is_equal).then_inc(sel_done, 1)
                j, h = behind(i, g, 3)
                if j.exists and h % BATCH == BATCH - 1:
                    w = h // BATCH
                    dve.wait_ge(ltt_done, j.count(2, w + 1))
                    first = 1 + w * BATCH * GROUP
                    dve.tensor_scalar(
                        logit[:, j.buf, :, first:first + BATCH * GROUP].rearrange("p h (v t) -> p t v h", t=GROUP),
                        ltt_ps.rearrange("p (t q) -> p t q", t=GROUP)[:, :, 0:BATCH * HEADS].rearrange(
                            "p t (v h) -> p t v h", h=HEADS),
                        ab_sb[:, 0:1], None, ALU.add).then_inc(logit_done, 1)
                b = i.shift(-1)
                if b.exists and g == 1:
                    dve.wait_ge(ends_tr, b.count(1, 1))
                    dve.tensor_copy(dts[:, :, :].rearrange("h a p -> h (a p)"), edge_first_ps).then_inc(ends_done, 1)
                    dve.wait_ge(ends_done, b.count(1, 1))
                    for n in range(2):
                        dve.tensor_tensor(penf[:, n, 1:P], dts[:, 1, 0:P - 1], dts[:, 1 - n, 1:P], ALU.subtract)
                    for n in range(2):
                        last = dve.tensor_tensor(penb[:, n, 0:P - 1], dts[:, n, 0:P - 1], dts[:, 0, 1:P], ALU.subtract)
                    last.then_inc(pens_done, 1)
                if b.exists and g == 2:
                    dve.wait_ge(logit_done, b.count(2, 2))
                    scans(b.buf).then_inc(scan_done, 1)
                if b.exists and g == 3:
                    dve.wait_ge(scan_tr, b.count(1, 1))
                    dve.wait_ge(pens_done, b.count(1, 1))
                    dve.tensor_tensor_scan(tf[:, :], penf[:, 0, :], edge_first_ps[:, 0:P], -BIG, ALU.add, ALU.max)
                    dve.tensor_tensor_scan(tb[:, ::-1], penb[:, 0, ::-1], edge_first_ps[:, P:2 * P][:, ::-1], -BIG,
                                           ALU.add, ALU.max).then_inc(tscan_done, 1)
                    dve.wait_ge(tscan_done, b.count(1, 1))
                    dve.tensor_tensor(carry[:, 0, 1:P], tf[:, 0:P - 1], penf[:, 1, 1:P], ALU.add)
                    dve.tensor_tensor(carry[:, 1, 0:P - 1], tb[:, 1:P], penb[:, 1, 0:P - 1], ALU.add).then_inc(carry_done, 1)
                if b.exists and g == 4:
                    dve.wait_ge(carry_tr, b.count(1, 1))
                    dve.tensor_copy(logit[:, b.buf, :, 0:FRAME:FRAME - 1].rearrange("p h a -> p a h"),
                                    carry_ps.rearrange("p (a h) -> p a h", a=2)).then_inc(carry_in, 1)
                    dve.wait_ge(carry_in, b.count(1, 1))
                    scans(b.buf).then_inc(rescan_done, 1)
                    dve.wait_ge(rescan_done, b.count(1, 1))
                    dve.tensor_tensor(top[:, :, :], fwd[:, :, 1:TILES + 1], bwd[:, :, 1:TILES + 1], ALU.max).then_inc(top_done, 1)
                    dve.wait_ge(top_done, b.count(1, 1))
                    dve.tensor_tensor(diff[:, :, :], logit[:, b.buf, :, 1:TILES + 1], top[:, :, :],
                                      ALU.subtract).then_inc(diff_done, 1)
                j, h = behind(i, g, 11)
                if j.exists:
                    dve.wait_ge(p_done, j.count(1, 1))
                    rows = s_buf[:, j.buf, GROUP * h:GROUP * (h + 1), :]
                    sent = rows[:, :, 0:D].rearrange("p j (h c) -> p j h c", h=HEADS)
                    dve.tensor_tensor(sent, sent, rows[:, :, D:ROW][:, :, :, None].broadcast_to([P, GROUP, HEADS, HD]),
                                      ALU.mult).then_inc(msg_done, 1)
                b = i.shift(-3)
                if b.exists and g == 0:
                    finish_a(b)
                if b.exists and g == 2:
                    finish_b(b)
                if i.exists:
                    dve.wait_ge(r_done, i.count(GROUPS, g + 1))
                    if i.positive(GROUPS, g - 1):
                        dve.wait_ge(score_done, i.count(GROUPS, g - 1))
                    dve.scalar_tensor_tensor(h_buf[:, par], e_buf[:, par], 0.5, z_ps[:, par, :, 0:COLS],
                                             ALU.subtract, ALU.mult).then_inc(h_done, 1)

            def body(i):
                for g in range(GROUPS):
                    slot(i, g)

            iterations(dve, body)


_INS = ['x', 'src', 'dst', 'L0_gnn_Wi', 'L0_gnn_bi', 'L0_gnn_Wj', 'L0_gnn_bj', 'L0_gnn_a_w', 'L0_gnn_a_b']
_SHAPES = {'L0_gnn_Wi': (D, D), 'L0_gnn_bi': (1, D), 'L0_gnn_Wj': (D, D), 'L0_gnn_bj': (1, D),
           'L0_gnn_a_w': (HD, 1), 'L0_gnn_a_b': (1, 1)}


def kernel(**inputs):
    import numpy as _np
    import concourse.bacc as _bacc
    from concourse import mybir as _mybir
    from concourse.bass_utils import run_bass_kernel_spmd as _run

    nc = _bacc.Bacc("TRN2", target_bir_lowering=False, num_devices=1)
    arrays, args = {}, []
    for name in _INS:
        a = _np.ascontiguousarray(inputs[name])
        a = a.reshape(_SHAPES.get(name, a.shape))
        arrays[f"in_{name}_dram"] = a
        args.append(nc.dram_tensor(f"in_{name}_dram", a.shape, _mybir.dt.from_np(a.dtype), kind="ExternalInput").ap())
    shape = arrays["in_x_dram"].shape
    args.append(nc.dram_tensor("out_0_dram", shape, F32, kind="ExternalOutput").ap())
    gnn_program(nc, *args)
    r = _run(nc, [arrays], core_ids=[0])
    return r.results[0]["out_0_dram"]
```

```python
from contextlib import ExitStack

import concourse.bass as bass
from concourse import mybir

F32 = mybir.dt.float32
F32R = mybir.dt.float32r
BF16 = mybir.dt.bfloat16
I32 = mybir.dt.int32
ALU = mybir.AluOpType
ACT = mybir.ActivationFunctionType

P = 128
D = 256
HEADS = 8
HD = D // HEADS
TILES = 18
GROUP = 3
GROUPS = TILES // GROUP
COLS = GROUP * P
BLOCK_EDGES = TILES * P
FRAME = TILES + 2
ROW = D + HEADS
XBUFS = 4
BATCH = 3
BIG = 1.0e30
STEP = 2.0 ** 90
NO_NODE = 1 << 14
E_MAX = 1.0e9
EPS = 1e-5


class Block_:

    def __init__(self, u, c, blocks):
        self.u, self.c, self.blocks = u, c, blocks
        self.fixed = isinstance(u, int)

    def shift(self, d):
        return Block_(self.u, self.c + d, self.blocks)

    @property
    def exists(self):
        if not self.fixed:
            assert self.c >= -3
            return True
        return 0 <= 3 * self.u + self.c < self.blocks

    @property
    def is_last(self):
        return self.fixed and 3 * self.u + self.c == self.blocks - 1

    @property
    def buf(self):
        return self.c % 3

    @property
    def index(self):
        return self.u * 3 + self.c

    def count(self, per_block, more=0):
        return self.u * (3 * per_block) + (self.c * per_block + more)

    def uses(self, per_use):
        return self.u * per_use + (self.c // 3 + 1) * per_use

    def positive(self, per_block, more=0):
        least = self.u if self.fixed else 1
        return (3 * least + self.c) * per_block + more > 0


def behind(i, g, lag):
    s = g - lag
    return i.shift(s // GROUPS), s % GROUPS


def gnn_program(nc, x, src, dst, wi, bi, wj, bj, aw, ab, out):
    n_nodes, n_edges = x.shape[0], src.shape[0]
    blocks = -(-n_nodes // P)
    last_rows = n_nodes - (blocks - 1) * P
    edge_tiles = -(-n_edges // P)
    bounds = blocks + 1
    assert bounds <= P and edge_tiles <= 2048 and blocks % 2 == 0

    s_dram = nc.dram_tensor("sent_rows", [blocks * P, D], F32).ap()
    r_dram = nc.dram_tensor("received_rows", [blocks * P, 2 * D], F32).ap()
    srcp = nc.dram_tensor("src_padded", [n_edges + BLOCK_EDGES], I32).ap()
    dstp = nc.dram_tensor("dst_padded", [edge_tiles * P + BLOCK_EDGES], I32).ap()
    ptr_dram = nc.dram_tensor("row_starts", [bounds], I32).ap()

    ctx = ExitStack()
    with ctx:
        def sb(name, shape, dt=F32):
            return ctx.enter_context(nc.sbuf_tensor(name, shape, dt))

        def sem(name):
            return ctx.enter_context(nc.semaphore(name))

        ident = sb("ident", [P, P])
        ident_b = sb("ident_b", [P, P], BF16)
        node_col = sb("node_col", [P, P])
        w_sb = sb("w_sb", [P, 2, 2 * D])
        bias = sb("bias", [P, 2 * D])
        aw_sb = sb("aw_sb", [P, 1])
        ab_sb = sb("ab_sb", [P, 1])
        score_w = sb("score_w", [P, BATCH, 2, 32])
        zero_row = sb("zero_row", [1, BLOCK_EDGES], I32)
        none_row = sb("none_row", [1, BLOCK_EDGES + P], I32)
        ones_row = sb("ones_row", [1, P])
        firsts_i = sb("firsts_i", [1, edge_tiles], I32)
        firsts = sb("firsts", [1, edge_tiles])
        bound_i = sb("bound_i", [P, 1], I32)
        bound = sb("bound", [P, 1])
        before = sb("before", [P, edge_tiles])
        n_tiles_before = sb("n_tiles_before", [P, 1])
        at_tile = sb("at_tile", [P, 1])
        at_tile_i = sb("at_tile_i", [P, 1], I32)
        edge_row = sb("edge_row", [P, P], I32)
        before_row = sb("before_row", [P, P])
        n_before = sb("n_before", [P, 1])
        starts_i = sb("starts_i", [P, 1], I32)
        starts = sb("starts", [1, bounds], I32)
        xt = sb("xt", [P, XBUFS, D])
        xT = sb("xT", [P, 2, 2, P])
        sr = sb("sr", [P, XBUFS, 2 * D])
        rhl = sb("rhl", [P, XBUFS, 2, D], F32R)
        src_i = sb("src_i", [P, 3, TILES], I32)
        dst_i = sb("dst_i", [P, 3, TILES], I32)
        s_buf = sb("s_buf", [P, 3, TILES, ROW])
        r_buf = sb("r_buf", [P, 3, 2, D], F32R)
        nbase = sb("nbase", [P, 3])
        dl = sb("dl", [P, 3, TILES])
        dlb = sb("dlb", [P, 3, TILES])
        sel = sb("sel", [P, 3, TILES, P])
        sel_b = sb("sel_b", [P, 2, GROUP, P], BF16)
        selT = sb("selT", [P, 2, COLS], F32R)
        e_buf = sb("e_buf", [P, 2, 2, COLS])
        h_buf = sb("h_buf", [P, 2, 2, COLS])
        lts = sb("lts", [32 * GROUP, P])
        logit = sb("logit", [P, 3, HEADS, FRAME])
        pen = sb("pen", [P, 3, HEADS * FRAME + 1])
        fwd = sb("fwd", [P, HEADS, FRAME])
        bwd = sb("bwd", [P, HEADS, FRAME])
        dts = sb("dts", [HEADS, 2, P])
        penf = sb("penf", [HEADS, 2, P])
        penb = sb("penb", [HEADS, 2, P])
        tf = sb("tf", [HEADS, P])
        tb = sb("tb", [HEADS, P])
        carry = sb("carry", [HEADS, 2, P])
        top = sb("top", [P, HEADS, TILES])
        diff = sb("diff", [P, HEADS, TILES])
        x_buf = sb("x_buf", [P, 3, D])
        den = sb("den", [P, HEADS])
        rden = sb("rden", [P, HEADS])
        y = sb("y", [P, D])
        yx = sb("yx", [P, D])
        stats = sb("stats", [P, 6])
        mv = sb("mv", [P, 2])
        eps_sb = sb("eps_sb", [P, 1])
        lnv = sb("lnv", [P, 1])
        rs0 = sb("rs0", [P, 1])
        nt = sb("nt", [P, 3])
        rs1 = sb("rs1", [P, 1])
        y_buf = sb("y_buf", [P, 3, D])

        z_ps = ctx.enter_context(nc.psum_tensor("z_ps", [P, 2, 2, 512], F32))
        pm = ctx.enter_context(nc.psum_tensor("pm", [P, 4, 512], F32))
        selT_ps = pm[:, 0, 0:COLS]
        acc_ps = pm[:, 1, 0:ROW]
        lt_ps = pm[0:32 * GROUP, 2, 0:P]
        misc = pm[:, 3, :]
        edge_first_ps = misc[0:HEADS, 0:2 * P]
        ltt_ps = misc[:, 256:256 + 32 * GROUP]
        carry_ps = misc[:, 384:384 + 2 * HEADS]

        def frame_flat(t, k):
            return t[:, k].rearrange("p h f -> p (h f)")

        s_const = sem("s_const")
        s_pad = sem("s_pad")
        s_first = sem("s_first")
        s_fill = sem("s_fill")
        s_pool_const = sem("s_pool_const")
        s_dve_const = sem("s_dve_const")
        s_firsts_f = sem("s_firsts_f")
        s_bc = sem("s_bc")
        s_at = sem("s_at")
        s_edge_row = sem("s_edge_row")
        s_starts_i = sem("s_starts_i")
        s_starts_d = sem("s_starts_d")
        s_starts = sem("s_starts")
        s_setup = sem("s_setup")
        s_xt = [sem(f"s_xt{a}") for a in range(XBUFS)]
        s_xtr = sem("s_xtr")
        s_xT = sem("s_xT")
        s_proj = sem("s_proj")
        s_sr = sem("s_sr")
        s_rhi = sem("s_rhi")
        s_rlo = sem("s_rlo")
        s_s_out = [sem(f"s_s_out{a}") for a in range(XBUFS)]
        s_r_out = [sem(f"s_r_out{a}") for a in range(XBUFS)]

        src_in = [sem(f"src_in{k}") for k in range(3)]
        dst_in = [sem(f"dst_in{k}") for k in range(3)]
        r_in = [sem(f"r_in{k}") for k in range(3)]
        x_in = [sem(f"x_in{k}") for k in range(3)]
        gathered = [[sem(f"gathered{k}_{g}") for g in range(GROUPS)] for k in range(3)]
        y_out = sem("y_out")
        y_free = sem("y_free")
        prepped = sem("prepped")
        prep_step = sem("prep_step")
        sel_done = sem("sel_done")
        sel_b_done = sem("sel_b_done")
        selT_tr = sem("selT_tr")
        selT_done = sem("selT_done")
        z_done = sem("z_done")
        exp_done = sem("exp_done")
        cut_done = sem("cut_done")
        sq_done = sem("sq_done")
        ln_done = sem("ln_done")
        r_done = sem("r_done")
        h_done = sem("h_done")
        score_done = sem("score_done")
        lt_done = sem("lt_done")
        ltt_done = sem("ltt_done")
        logit_done = sem("logit_done")
        ends_tr = sem("ends_tr")
        ends_done = sem("ends_done")
        pens_done = sem("pens_done")
        scan_done = sem("scan_done")
        scan_tr = sem("scan_tr")
        tscan_done = sem("tscan_done")
        carry_done = sem("carry_done")
        carry_tr = sem("carry_tr")
        carry_in = sem("carry_in")
        rescan_done = sem("rescan_done")
        top_done = sem("top_done")
        diff_done = sem("diff_done")
        p_done = sem("p_done")
        msg_done = sem("msg_done")
        out_done = sem("out_done")
        den_done = sem("den_done")
        rden_done = sem("rden_done")
        acc_read = sem("acc_read")
        yx_done = sem("yx_done")
        stats_done = sem("stats_done")
        mv_done = sem("mv_done")
        lnv_done = sem("lnv_done")
        rs0_done = sem("rs0_done")
        newton = sem("newton")
        y_done = sem("y_done")
        sp_passed = sem("sp_passed")
        pool_passed = sem("pool_passed")
        dve_passed = sem("dve_passed")

        block = ctx.enter_context(nc.Block())

        def iterations(eng, body, first=-1, last=None):
            last = blocks + 3 if last is None else last
            turns = (blocks - 2) // 3
            for c in range(first, min(3, last + 1)):
                body(Block_(0, c, blocks))
            if turns > 1:
                with eng.Fori(1, turns) as u:
                    for c in range(3):
                        body(Block_(u, c, blocks))
            for c in range(3 * max(turns, 1), last + 1):
                body(Block_(0, c, blocks))

        def projected_tiles(eng, body):
            turns = (blocks - 1) // XBUFS
            for a in range(XBUFS):
                body(0, a)
            if turns > 1:
                with eng.Fori(1, turns) as v:
                    for a in range(XBUFS):
                        body(v, a)
            for a in range(blocks - XBUFS * turns):
                body(turns, a)

        def past(v, a, n):
            return (XBUFS * v + a if isinstance(v, int) else XBUFS + a) >= n

        def stored(a):
            return 16 * -(-(blocks - a) // XBUFS)

        @block.sync
        def _(sp):
            sp.dma_start(firsts_i[0:1, :], dst.rearrange("(a e) -> a e", a=1)[:, 0:n_edges:P],
                         allow_slow_non_contiguous=True).then_inc(s_first, 16)
            for k in range(2):
                sp.dma_start(w_sb[:, k, 0:D], wi[k * P:(k + 1) * P, :]).then_inc(s_const, 16)
                sp.dma_start(w_sb[:, k, D:2 * D], wj[k * P:(k + 1) * P, :]).then_inc(s_const, 16)
            sp.dma_start(bias[:, 0:D], bi.broadcast_to([P, D])).then_inc(s_const, 16)
            sp.dma_start(bias[:, D:2 * D], bj.broadcast_to([P, D])).then_inc(s_const, 16)
            for g in range(P // HD):
                sp.dma_start(aw_sb[g * HD:(g + 1) * HD, :], aw).then_inc(s_const, 16)
            sp.dma_start(ab_sb[:, :], ab.broadcast_to([P, 1])).then_inc(s_const, 16)
            sp.dma_start(srcp[0:n_edges], src).then_inc(s_pad, 16)
            sp.dma_start(dstp[0:n_edges], dst).then_inc(s_pad, 16)
            sp.wait_ge(s_fill, 2)
            sp.dma_start(srcp[n_edges:n_edges + BLOCK_EDGES].rearrange("(a e) -> a e", a=1),
                         zero_row[:, :]).then_inc(s_pad, 16)
            tail = edge_tiles * P + BLOCK_EDGES - n_edges
            sp.dma_start(dstp[n_edges:n_edges + tail].rearrange("(a e) -> a e", a=1),
                         none_row[:, 0:tail]).then_inc(s_pad, 16)

            def load_rows(v, a):
                rows = last_rows if isinstance(v, int) and XBUFS * v + a == blocks - 1 else P
                if past(v, a, XBUFS):
                    sp.wait_ge(s_xtr, v * XBUFS + (a - XBUFS + 1))
                    sp.sem_inc(sp_passed, 1)
                sp.dma_start(xt[0:rows, a, :], x[bass.ds(v * (XBUFS * P) + a * P, rows), :]).then_inc(s_xt[a], 16)

            def store_r(v, a):
                sp.wait_ge(s_rlo, v * XBUFS + (a + 1))
                sp.sem_inc(sp_passed, 1)
                sp.dma_start(r_dram[bass.ds(v * (XBUFS * P) + a * P, P), :],
                             rhl[:, a].bitcast(F32).rearrange("p a b -> p (a b)")).then_inc(s_r_out[a], 16)

            def project(v, a):
                load_rows(v, a)
                if past(v, a, XBUFS):
                    store_r(v - 1, a)

            projected_tiles(sp, project)
            last_stores = [(t // XBUFS, t % XBUFS) for t in range(blocks - XBUFS, blocks)]
            sp.wait_ge(s_starts_i, 1)
            sp.dma_start(ptr_dram.rearrange("(b a) -> b a", a=1), starts_i[0:bounds, :]).then_inc(s_starts_d, 16)
            for v, a in last_stores[:2]:
                store_r(v, a)
            sp.wait_ge(s_starts_d, 16)
            sp.dma_start(starts[0:1, :], ptr_dram.rearrange("(a b) -> a b", a=1)).then_inc(s_starts, 16)
            for v, a in last_stores[2:]:
                store_r(v, a)
            sp.wait_ge(s_starts, 16)
            sp.wait_ge(s_pad, 64)
            for a in range(XBUFS):
                sp.wait_ge(s_r_out[a], stored(a) - 16)
            sp.sem_inc(y_free, 3)

            def load(j):
                old = j.shift(-3)
                start = sp.value_load(starts[0:1, bass.ds(j.index, 1)], min_val=0, max_val=n_edges)
                first_row = j.count(P)
                if old.exists:
                    for g in range(GROUPS):
                        sp.wait_ge(gathered[old.buf][g], old.uses(16 * GROUP))
                    sp.sem_inc(sp_passed, 1)
                    sp.wait_ge(prepped, old.count(1, 1))
                    sp.sem_inc(sp_passed, 1)
                    sp.wait_ge(z_done, old.count(GROUPS, GROUPS))
                    sp.sem_inc(sp_passed, 1)
                k = j.buf
                sp.dma_start(src_i[:, k, :], srcp[bass.ds(start, BLOCK_EDGES)].rearrange(
                    "(p j) -> p j", j=TILES)).then_inc(src_in[k], 16)
                sp.dma_start(dst_i[:, k, :], dstp[bass.ds(start, BLOCK_EDGES)].rearrange(
                    "(p j) -> p j", j=TILES)).then_inc(dst_in[k], 16)
                sp.dma_start(r_buf[:, k].bitcast(F32).rearrange("p a b -> p (a b)"),
                             r_dram[bass.ds(first_row, P), :]).then_inc(r_in[k], 16)

            def load_x(i):
                old, k = i.shift(-3), i.buf
                rows = last_rows if i.is_last else P
                first_row = i.count(P)
                if old.exists:
                    sp.wait_ge(yx_done, old.count(1, 1))
                    sp.sem_inc(sp_passed, 1)
                sp.dma_start(x_buf[0:rows, k, :], x[bass.ds(first_row, rows), :]).then_inc(x_in[k], 16)

            def store_y(b):
                rows = last_rows if b.is_last else P
                first_row = b.count(P)
                sp.wait_ge(y_done, b.count(1, 1))
                sp.sem_inc(sp_passed, 1)
                sp.dma_start(out[bass.ds(first_row, rows), :], y_buf[0:rows, b.buf, :]).then_inc(y_out, 16)
                sp.wait_ge(y_out, b.count(16, 16))
                sp.sem_inc(y_free, 1)

            load(Block_(0, 0, blocks))
            for a in range(XBUFS):
                sp.wait_ge(s_r_out[a], stored(a))

            def body(i):
                if i.shift(2).exists:
                    load(i.shift(2))
                if i.exists:
                    load_x(i)
                if i.shift(-3).exists:
                    store_y(i.shift(-3))

            iterations(sp, body)

        @block.gpsimd
        def _(pool):
            pool.memset(zero_row[:, :], 0).then_inc(s_fill, 1)
            pool.memset(none_row[:, :], NO_NODE).then_inc(s_fill, 1)
            pool.memset(ones_row[:, :], 1.0).then_inc(s_pool_const, 1)
            pool.memset(ident[:, :], 0.0).then_inc(s_pool_const, 1)
            pool.iota(node_col[:, :], pattern=[[1, P]], base=0, channel_multiplier=0,
                      allow_small_or_imprecise_dtypes=True).then_inc(s_pool_const, 1)
            pool.iota(bound_i[:, :], pattern=[[0, 1]], base=0, channel_multiplier=P).then_inc(s_pool_const, 1)
            pool.wait_ge(s_pool_const, 4)
            pool.affine_select(out=ident[:, :], in_=ident[:, :], compare_op=ALU.not_equal, fill=1.0,
                               base=0, pattern=[[-1, P]], channel_multiplier=1).then_inc(s_pool_const, 1)
            pool.wait_ge(s_pad, 64)
            pool.wait_ge(s_at, 1)
            pool.indirect_dma_start(
                out=edge_row[0:bounds, :], out_offset=None,
                in_=dstp[0:edge_tiles * P].rearrange("(t e) -> t e", e=P),
                in_offset=bass.IndirectOffsetOnAxis(ap=at_tile_i[0:bounds, 0:1], axis=0),
            ).then_inc(s_edge_row, 16)

            def store_s(v, a):
                pool.wait_ge(s_sr, v * XBUFS + (a + 1))
                pool.sem_inc(pool_passed, 1)
                pool.dma_start(s_dram[bass.ds(v * (XBUFS * P) + a * P, P), :],
                               sr[:, a, 0:D]).then_inc(s_s_out[a], 16)

            projected_tiles(pool, store_s)
            for a in range(XBUFS):
                pool.wait_ge(s_s_out[a], stored(a))

            def body(j):
                k, old = j.buf, j.shift(-3)
                pool.wait_ge(src_in[k], j.uses(16))
                pool.sem_inc(pool_passed, 1)
                for g in range(GROUPS):
                    if old.exists:
                        pool.wait_ge(out_done, old.count(GROUPS, g + 1))
                        pool.sem_inc(pool_passed, 1)
                    for t in range(GROUP * g, GROUP * (g + 1)):
                        pool.indirect_dma_start(
                            out=s_buf[:, k, t, 0:D], out_offset=None, in_=s_dram,
                            in_offset=bass.IndirectOffsetOnAxis(ap=src_i[:, k, t:t + 1], axis=0),
                        ).then_inc(gathered[k][g], 16)

            iterations(pool, body, first=0, last=blocks - 1)

        @block.scalar
        def _(act):
            act.preload_act_table_set("natural_log_exp_and_others")

            def project(v, a):
                act.wait_ge(s_xtr, v * XBUFS + (a + 1))
                if past(v, a, 2):
                    act.wait_ge(s_proj, v * XBUFS + (a - 1))
                act.activation(xT[:, a % 2].rearrange("p k n -> p (k n)"), z_ps[:, a % 2, 0, 0:2 * P],
                               ACT.Copy).then_inc(s_xT, 1)
                if past(v, a, 1):
                    split_hi(v, a - 1)

            def split_hi(v, a):
                act.wait_ge(s_sr, v * XBUFS + (a + 1))
                if past(v, a, XBUFS):
                    act.wait_ge(s_r_out[a % XBUFS], (v + a // XBUFS) * 16)
                act.activation(rhl[:, a % XBUFS, 0, :], sr[:, a % XBUFS, D:2 * D], ACT.Copy).then_inc(s_rhi, 1)

            projected_tiles(act, project)
            split_hi(0, blocks - 1)

            def slot(i, g):
                par = g % 2
                b = i.shift(-1)
                if g == GROUPS - 1 and b.exists:
                    act.wait_ge(diff_done, b.count(1, 1))
                    act.activation(s_buf[:, b.buf, :, D:ROW].rearrange("p j h -> p h j"), diff[:, :, :],
                                   ACT.Exp).then_inc(p_done, 1)
                j, h = behind(i, g, 2)
                if j.exists and h % BATCH == BATCH - 1:
                    w = h // BATCH
                    act.wait_ge(score_done, j.count(GROUPS, h + 1))
                    if j.positive(2, w):
                        act.wait_ge(ltt_done, j.count(2, w))
                    act.activation(lts[:, :], lt_ps, ACT.Copy).then_inc(lt_done, 1)
                if i.exists:
                    act.wait_ge(z_done, i.count(GROUPS, g + 1))
                    act.activation(e_buf[:, par], z_ps[:, par, :, 0:COLS], ACT.Exp).then_inc(exp_done, 1)
                j, h = behind(i, g, -2)
                if j.exists:
                    act.wait_ge(selT_tr, j.count(GROUPS, h + 1))
                    act.activation(selT[:, par, :], selT_ps, ACT.Copy).then_inc(selT_done, 1)
                j, h = behind(i, g, -3)
                if j.exists:
                    act.wait_ge(sel_done, j.count(GROUPS, h + 1))
                    if j.positive(GROUPS, h - 1):
                        act.wait_ge(selT_tr, j.count(GROUPS, h - 1))
                    act.activation(sel_b[:, 1 - par], sel[:, j.buf, GROUP * h:GROUP * (h + 1), :],
                                   ACT.Copy).then_inc(sel_b_done, 1)
                if i.exists:
                    act.wait_ge(cut_done, i.count(GROUPS, g + 1))
                    act.activation(e_buf[:, par], e_buf[:, par], ACT.Square, bias=1.0).then_inc(sq_done, 1)
                    act.wait_ge(sq_done, i.count(GROUPS, g + 1))
                    act.activation(e_buf[:, par], e_buf[:, par], ACT.Ln, bias=1.0).then_inc(ln_done, 1)
                    act.wait_ge(ln_done, i.count(GROUPS, g + 1))
                    act.activation(e_buf[:, par], e_buf[:, par], ACT.Exp, scale=-1.0).then_inc(r_done, 1)
                b = i.shift(-3)
                if g == 1 and b.exists:
                    act.wait_ge(mv_done, b.count(1, 1))
                    act.activation(lnv[:, :], mv[:, 1:2], ACT.Ln, bias=eps_sb[:, 0:1]).then_inc(lnv_done, 1)
                    act.wait_ge(lnv_done, b.count(1, 1))
                    act.activation(rs0[:, :], lnv[:, :], ACT.Exp, scale=-0.5).then_inc(rs0_done, 1)

            def body(i):
                for g in range(GROUPS):
                    slot(i, g)

            iterations(act, body)

        @block.tensor
        def _(pe):
            pe.wait_ge(s_pool_const, 5)
            pe.wait_ge(s_firsts_f, 1)
            for c in range(0, edge_tiles, 512):
                m = min(512, edge_tiles - c)
                last = pe.matmul(pm[:, c // 512, 0:m], ones_row[0:1, :], firsts[0:1, c:c + m],
                                 start=True, stop=True)
            last.then_inc(s_bc, 1)

            def product(v, a):
                pe.wait_ge(s_xT, v * XBUFS + (a + 1))
                if past(v, a, 2):
                    pe.wait_ge(s_sr, v * XBUFS + (a - 1))
                for k in range(2):
                    last = pe.matmul(z_ps[:, a % 2, 1, :], xT[:, a % 2, k, :], w_sb[:, k, :], start=k == 0, stop=k == 1)
                last.then_inc(s_proj, 1)

            def project(v, a):
                pe.wait_ge(s_xt[a], v * 16 + 16)
                if past(v, a, 2):
                    pe.wait_ge(s_xT, v * XBUFS + (a - 1))
                for k in range(2):
                    last = pe.transpose(z_ps[:, a % 2, 0, k * P:(k + 1) * P], xt[:, a, k * P:(k + 1) * P], ident[:, :])
                last.then_inc(s_xtr, 1)
                if past(v, a, 1):
                    product(v, a - 1)

            pe.wait_ge(s_const, 16 * (7 + P // HD))
            projected_tiles(pe, project)
            product(0, blocks - 1)
            pe.wait_ge(s_setup, 1)
            pe.wait_ge(s_sr, blocks)

            def slot(i, g):
                par = g % 2
                if i.exists:
                    k = i.buf
                    pe.wait_ge(selT_done, i.count(GROUPS, g + 1))
                    if g == 0:
                        pe.wait_ge(r_in[k], i.uses(16))
                    if i.positive(GROUPS, g - 1):
                        pe.wait_ge(h_done, i.count(GROUPS, g - 1))
                    pe.wait_ge(gathered[k][g], i.uses(16 * GROUP))
                    for hf in range(2):
                        f = slice(hf * P, (hf + 1) * P)
                        for part in range(2):
                            pe.matmul(z_ps[:, par, hf, 0:COLS], r_buf[:, k, part, f], selT[:, par, :],
                                      start=part == 0, stop=False)
                        for t in range(GROUP):
                            last = pe.matmul(z_ps[:, par, hf, t * P:(t + 1) * P], s_buf[:, k, GROUP * g + t, f],
                                             ident[:, :], start=False, stop=t == GROUP - 1)
                    last.then_inc(z_done, 1)
                j, h = behind(i, g, -2)
                if j.exists:
                    pe.wait_ge(sel_b_done, j.count(GROUPS, h + 1))
                    if j.positive(GROUPS, h):
                        pe.wait_ge(selT_done, j.count(GROUPS, h))
                    for t in range(GROUP):
                        last = pe.matmul(selT_ps[:, t * P:(t + 1) * P], sel_b[:, par, t, :], ident_b[:, :],
                                         start=True, stop=True)
                    last.then_inc(selT_tr, 1)
                j, h = behind(i, g, 3)
                if j.exists and h % BATCH == BATCH - 1:
                    w = h // BATCH
                    pe.wait_ge(lt_done, j.count(2, w + 1))
                    if w == 1:
                        pe.wait_ge(ends_done, j.count(1, 1))
                    elif j.positive(1):
                        pe.wait_ge(carry_in, j.count(1))
                    pe.transpose(ltt_ps, lts[:, :], ident[0:32 * GROUP, 0:32 * GROUP]).then_inc(ltt_done, 1)
                b = i.shift(-1)
                if b.exists and g == 0:
                    pe.wait_ge(prepped, b.count(1, 1))
                    pe.wait_ge(logit_done, b.count(2, 1))
                    for n, j_ in enumerate((0, TILES - 1)):
                        last = pe.matmul(edge_first_ps[:, n * P:(n + 1) * P],
                                         dlb[:, b.buf, j_:j_ + 1].broadcast_to([P, HEADS]), ident[:, :],
                                         start=True, stop=True)
                    last.then_inc(ends_tr, 1)
                if b.exists and g == 3:
                    pe.wait_ge(scan_done, b.count(1, 1))
                    pe.matmul(edge_first_ps[:, 0:P], fwd[:, :, TILES], ident[:, :], start=True, stop=True)
                    pe.matmul(edge_first_ps[:, P:2 * P], bwd[:, :, 1], ident[:, :],
                              start=True, stop=True).then_inc(scan_tr, 1)
                if b.exists and g == 4:
                    pe.wait_ge(carry_done, b.count(1, 1))
                    for n in range(2):
                        last = pe.matmul(carry_ps[:, n * HEADS:(n + 1) * HEADS], carry[:, n, :],
                                         ident[0:HEADS, 0:HEADS], start=True, stop=True)
                    last.then_inc(carry_tr, 1)
                j, h = behind(i, g, 12)
                if j.exists:
                    pe.wait_ge(msg_done, j.count(GROUPS, h + 1))
                    if h == 0 and j.positive(1):
                        pe.wait_ge(acc_read, j.count(1))
                    for t in range(GROUP * h, GROUP * (h + 1)):
                        last = pe.matmul(acc_ps, sel[:, j.buf, t, :], s_buf[:, j.buf, t, :],
                                         start=t == 0, stop=t == TILES - 1)
                    last.then_inc(out_done, 1)
                j, h = behind(i, g, 1)
                if j.exists:
                    w, v = h // BATCH, h % BATCH
                    pe.wait_ge(h_done, j.count(GROUPS, h + 1))
                    if v == 0 and j.positive(2, w):
                        pe.wait_ge(lt_done, j.count(2, w))
                    for hf in range(2):
                        for t in range(GROUP):
                            last = pe.matmul(lt_ps[32 * t:32 * t + 32, :], score_w[:, v, hf, :],
                                             h_buf[:, 1 - par, hf, t * P:(t + 1) * P],
                                             start=v == 0 and hf == 0, stop=v == BATCH - 1 and hf == 1,
                                             tile_position=(0, 32 * t))
                    last.then_inc(score_done, 1)

            def body(i):
                for g in range(GROUPS):
                    slot(i, g)

            iterations(pe, body)

        @block.vector
        def _(dve):
            dve.memset(score_w[:, :, :, :], 0.0).then_inc(s_dve_const, 1)
            dve.memset(pen[:, :, :], 0.0).then_inc(s_dve_const, 1)
            dve.memset(eps_sb[:, :], EPS).then_inc(s_dve_const, 1)
            dve.memset(carry[:, :, :], -BIG).then_inc(s_dve_const, 1)
            dve.memset(penf[:, :, :], 0.0).then_inc(s_dve_const, 1)
            dve.memset(penb[:, :, :], 0.0).then_inc(s_dve_const, 1)
            for k in range(3):
                dve.memset(nbase[:, k:k + 1], -float(P * k)).then_inc(s_dve_const, 1)
            dve.wait_ge(s_dve_const, 9)
            for k in range(3):
                last = dve.memset(pen[:, k, 0:HEADS * FRAME + 1:FRAME], -BIG)
            last.then_inc(s_dve_const, 1)

            dve.wait_ge(s_first, 16)
            dve.tensor_copy(firsts[0:1, :], firsts_i[0:1, :]).then_inc(s_firsts_f, 1)
            dve.wait_ge(s_pool_const, 5)
            dve.tensor_copy(bound[:, :], bound_i[:, :]).then_inc(s_firsts_f, 1)
            dve.tensor_copy(ident_b[:, :], ident[:, :])
            dve.wait_ge(s_bc, 1)
            dve.wait_ge(s_firsts_f, 2)
            dve.tensor_scalar(before[:, :], pm[:, :, :].rearrange("p a b -> p (a b)")[:, 0:edge_tiles],
                              bound[:, 0:1], None, ALU.is_lt).then_inc(s_firsts_f, 1)
            dve.wait_ge(s_firsts_f, 3)
            dve.reduce_sum(n_tiles_before[:, :], before[:, :], mybir.AxisListType.X).then_inc(s_firsts_f, 1)
            dve.wait_ge(s_firsts_f, 4)
            dve.tensor_scalar(at_tile[:, :], n_tiles_before[:, :], -1.0, 0.0, ALU.add, ALU.max).then_inc(s_firsts_f, 1)
            dve.wait_ge(s_firsts_f, 5)
            dve.tensor_copy(at_tile_i[:, :], at_tile[:, :]).then_inc(s_at, 1)

            dve.wait_ge(s_edge_row, 16)
            dve.tensor_scalar(before_row[0:bounds, :], edge_row[0:bounds, :], bound[0:bounds, 0:1], None,
                              ALU.is_lt).then_inc(s_firsts_f, 1)
            dve.wait_ge(s_firsts_f, 6)
            dve.reduce_sum(n_before[0:bounds, :], before_row[0:bounds, :], mybir.AxisListType.X).then_inc(s_firsts_f, 1)
            dve.wait_ge(s_firsts_f, 7)
            dve.scalar_tensor_tensor(starts_i[0:bounds, :], at_tile[0:bounds, :], float(P), n_before[0:bounds, :],
                                     ALU.mult, ALU.add).then_inc(s_starts_i, 1)
            dve.wait_ge(s_const, 16 * (7 + P // HD))
            for hf in range(2):
                for q in range(P // HD):
                    for v in range(BATCH):
                        at = v * HEADS + hf * (P // HD) + q
                        last = dve.tensor_scalar(score_w[q * HD:(q + 1) * HD, v, hf, at:at + 1],
                                                 aw_sb[q * HD:(q + 1) * HD, :], -2.0, None, ALU.mult)
            last.then_inc(s_setup, 1)

            def project(v, a):
                dve.wait_ge(s_proj, v * XBUFS + (a + 1))
                if past(v, a, XBUFS):
                    dve.wait_ge(s_s_out[a], v * 16)
                dve.tensor_tensor(sr[:, a, :], z_ps[:, a % 2, 1, :], bias[:, :], ALU.add).then_inc(s_sr, 1)
                if past(v, a, 1):
                    split_lo(v, a - 1)

            def split_lo(v, a):
                dve.wait_ge(s_rhi, v * XBUFS + (a + 1))
                dve.tensor_tensor(rhl[:, a % XBUFS, 1, :], sr[:, a % XBUFS, D:2 * D],
                                  rhl[:, a % XBUFS, 0, :].bitcast(F32), ALU.subtract).then_inc(s_rlo, 1)

            projected_tiles(dve, project)
            split_lo(0, blocks - 1)

            def prep(j):
                k = j.buf
                dve.wait_ge(dst_in[k], j.uses(16))
                dve.tensor_scalar(dl[:, k, :], dst_i[:, k, :], nbase[:, k:k + 1], None, ALU.add).then_inc(prep_step, 1)
                dve.memset(logit[:, k, :, 0:FRAME:FRAME - 1], -BIG)
                dve.wait_ge(prep_step, j.count(3, 1))
                dve.tensor_scalar(dlb[:, k, :], dl[:, k, :], STEP, None, ALU.mult).then_inc(prep_step, 1)
                dve.tensor_scalar(nbase[:, k:k + 1], nbase[:, k:k + 1], -3.0 * P, None, ALU.add).then_inc(prep_step, 1)
                dve.wait_ge(prep_step, j.count(3, 3))
                dve.tensor_tensor(
                    pen[:, k, 0:HEADS * FRAME].rearrange("p (h f) -> p h f", f=FRAME)[:, :, 2:TILES + 1],
                    dlb[:, k, None, 0:TILES - 1].broadcast_to([P, HEADS, TILES - 1]),
                    dlb[:, k, None, 1:TILES].broadcast_to([P, HEADS, TILES - 1]), ALU.subtract).then_inc(prepped, 1)

            def scans(k):
                dve.tensor_tensor_scan(fwd[:, :, :].rearrange("p h f -> p (h f)"), pen[:, k, 0:HEADS * FRAME],
                                       frame_flat(logit, k), -BIG, ALU.add, ALU.max)
                return dve.tensor_tensor_scan(bwd[:, :, :].rearrange("p h f -> p (h f)")[:, ::-1],
                                              pen[:, k, 1:HEADS * FRAME + 1][:, ::-1],
                                              frame_flat(logit, k)[:, ::-1], -BIG, ALU.add, ALU.max)

            def divide(b):
                dve.wait_ge(out_done, b.count(GROUPS, GROUPS))
                dve.tensor_scalar(den[:, :], acc_ps[:, D:ROW], 1e-30, None, ALU.max).then_inc(den_done, 1)
                dve.wait_ge(den_done, b.count(1, 1))
                dve.reciprocal(rden[:, :], den[:, :]).then_inc(rden_done, 1)
                dve.wait_ge(rden_done, b.count(1, 1))
                dve.tensor_tensor(y[:, :].rearrange("p (h c) -> p h c", h=HEADS),
                                  acc_ps[:, 0:D].rearrange("p (h c) -> p h c", h=HEADS),
                                  rden[:, :, None].broadcast_to([P, HEADS, HD]), ALU.mult).then_inc(acc_read, 1)

            def moments(b):
                k = b.buf
                dve.wait_ge(acc_read, b.count(1, 1))
                dve.wait_ge(x_in[k], b.uses(16))
                dve.tensor_tensor(yx[:, :], y[:, :], x_buf[:, k, :], ALU.add).then_inc(yx_done, 1)
                dve.wait_ge(yx_done, b.count(1, 1))
                dve.bn_stats(stats[:, :], yx[:, :]).then_inc(stats_done, 1)
                dve.wait_ge(stats_done, b.count(1, 1))
                dve.sem_inc(dve_passed, 1)
                dve.bn_aggr(mv[:, :], stats[:, :]).then_inc(mv_done, 1)

            def normalize(b):
                dve.wait_ge(rs0_done, b.count(1, 1))
                dve.scalar_tensor_tensor(nt[:, 0:1], mv[:, 1:2], EPS, rs0[:, :], ALU.add, ALU.mult).then_inc(newton, 1)
                dve.wait_ge(newton, b.count(4, 1))
                dve.tensor_tensor(nt[:, 1:2], nt[:, 0:1], rs0[:, :], ALU.mult).then_inc(newton, 1)
                dve.wait_ge(newton, b.count(4, 2))
                dve.tensor_scalar(nt[:, 2:3], nt[:, 1:2], -0.5, 1.5, ALU.mult, ALU.add).then_inc(newton, 1)
                dve.wait_ge(newton, b.count(4, 3))
                dve.tensor_tensor(rs1[:, :], nt[:, 2:3], rs0[:, :], ALU.mult).then_inc(newton, 1)
                dve.wait_ge(newton, b.count(4, 4))
                dve.wait_ge(y_free, b.count(1, 1))
                dve.tensor_scalar(y_buf[:, b.buf, :], yx[:, :], mv[:, 0:1], rs1[:, 0:1], ALU.subtract,
                                  ALU.mult).then_inc(y_done, 1)

            def slot(i, g):
                par = g % 2
                if i.exists:
                    dve.wait_ge(exp_done, i.count(GROUPS, g + 1))
                    dve.tensor_scalar(e_buf[:, par], e_buf[:, par], E_MAX, None, ALU.min).then_inc(cut_done, 1)
                if g == 0 and i.shift(1).exists:
                    prep(i.shift(1))
                j, h = behind(i, g, -5)
                if j.exists:
                    old = j.shift(-3)
                    dve.wait_ge(prepped, j.count(1, 1))
                    if old.exists:
                        dve.wait_ge(out_done, old.count(GROUPS, h + 1))
                    dve.tensor_tensor(
                        sel[:, j.buf, GROUP * h:GROUP * (h + 1), :],
                        node_col[:, None, :].broadcast_to([P, GROUP, P]),
                        dl[:, j.buf, GROUP * h:GROUP * (h + 1), None].broadcast_to([P, GROUP, P]),
                        ALU.is_equal).then_inc(sel_done, 1)
                j, h = behind(i, g, 3)
                if j.exists and h % BATCH == BATCH - 1:
                    w = h // BATCH
                    dve.wait_ge(ltt_done, j.count(2, w + 1))
                    first = 1 + w * BATCH * GROUP
                    dve.tensor_scalar(
                        logit[:, j.buf, :, first:first + BATCH * GROUP].rearrange("p h (v t) -> p t v h", t=GROUP),
                        ltt_ps.rearrange("p (t q) -> p t q", t=GROUP)[:, :, 0:BATCH * HEADS].rearrange(
                            "p t (v h) -> p t v h", h=HEADS),
                        ab_sb[:, 0:1], None, ALU.add).then_inc(logit_done, 1)
                b = i.shift(-1)
                if b.exists and g == 1:
                    dve.wait_ge(ends_tr, b.count(1, 1))
                    dve.tensor_copy(dts[:, :, :].rearrange("h a p -> h (a p)"), edge_first_ps).then_inc(ends_done, 1)
                    dve.wait_ge(ends_done, b.count(1, 1))
                    for n in range(2):
                        dve.tensor_tensor(penf[:, n, 1:P], dts[:, 1, 0:P - 1], dts[:, 1 - n, 1:P], ALU.subtract)
                    for n in range(2):
                        last = dve.tensor_tensor(penb[:, n, 0:P - 1], dts[:, n, 0:P - 1], dts[:, 0, 1:P], ALU.subtract)
                    last.then_inc(pens_done, 1)
                if b.exists and g == 2:
                    dve.wait_ge(logit_done, b.count(2, 2))
                    scans(b.buf).then_inc(scan_done, 1)
                if b.exists and g == 3:
                    dve.wait_ge(scan_tr, b.count(1, 1))
                    dve.wait_ge(pens_done, b.count(1, 1))
                    dve.tensor_tensor_scan(tf[:, :], penf[:, 0, :], edge_first_ps[:, 0:P], -BIG, ALU.add, ALU.max)
                    dve.tensor_tensor_scan(tb[:, ::-1], penb[:, 0, ::-1], edge_first_ps[:, P:2 * P][:, ::-1], -BIG,
                                           ALU.add, ALU.max).then_inc(tscan_done, 1)
                    dve.wait_ge(tscan_done, b.count(1, 1))
                    dve.tensor_tensor(carry[:, 0, 1:P], tf[:, 0:P - 1], penf[:, 1, 1:P], ALU.add)
                    dve.tensor_tensor(carry[:, 1, 0:P - 1], tb[:, 1:P], penb[:, 1, 0:P - 1], ALU.add).then_inc(carry_done, 1)
                if b.exists and g == 4:
                    dve.wait_ge(carry_tr, b.count(1, 1))
                    dve.tensor_copy(logit[:, b.buf, :, 0:FRAME:FRAME - 1].rearrange("p h a -> p a h"),
                                    carry_ps.rearrange("p (a h) -> p a h", a=2)).then_inc(carry_in, 1)
                    dve.wait_ge(carry_in, b.count(1, 1))
                    scans(b.buf).then_inc(rescan_done, 1)
                    dve.wait_ge(rescan_done, b.count(1, 1))
                    dve.tensor_tensor(top[:, :, :], fwd[:, :, 1:TILES + 1], bwd[:, :, 1:TILES + 1], ALU.max).then_inc(top_done, 1)
                    dve.wait_ge(top_done, b.count(1, 1))
                    dve.tensor_tensor(diff[:, :, :], logit[:, b.buf, :, 1:TILES + 1], top[:, :, :],
                                      ALU.subtract).then_inc(diff_done, 1)
                j, h = behind(i, g, 11)
                if j.exists:
                    dve.wait_ge(p_done, j.count(1, 1))
                    rows = s_buf[:, j.buf, GROUP * h:GROUP * (h + 1), :]
                    sent = rows[:, :, 0:D].rearrange("p j (h c) -> p j h c", h=HEADS)
                    dve.tensor_tensor(sent, sent, rows[:, :, D:ROW][:, :, :, None].broadcast_to([P, GROUP, HEADS, HD]),
                                      ALU.mult).then_inc(msg_done, 1)
                b = i.shift(-2)
                if b.exists and g == GROUPS - 1:
                    divide(b)
                b = i.shift(-3)
                if b.exists and g == 0:
                    moments(b)
                if b.exists and g == 2:
                    normalize(b)
                if i.exists:
                    dve.wait_ge(r_done, i.count(GROUPS, g + 1))
                    if i.positive(GROUPS, g - 1):
                        dve.wait_ge(score_done, i.count(GROUPS, g - 1))
                    dve.scalar_tensor_tensor(h_buf[:, par], e_buf[:, par], 0.5, z_ps[:, par, :, 0:COLS],
                                             ALU.subtract, ALU.mult).then_inc(h_done, 1)

            def body(i):
                for g in range(GROUPS):
                    slot(i, g)

            iterations(dve, body)


_INS = ['x', 'src', 'dst', 'L0_gnn_Wi', 'L0_gnn_bi', 'L0_gnn_Wj', 'L0_gnn_bj', 'L0_gnn_a_w', 'L0_gnn_a_b']
_SHAPES = {'L0_gnn_Wi': (D, D), 'L0_gnn_bi': (1, D), 'L0_gnn_Wj': (D, D), 'L0_gnn_bj': (1, D),
           'L0_gnn_a_w': (HD, 1), 'L0_gnn_a_b': (1, 1)}


def kernel(**inputs):
    import numpy as _np
    import concourse.bacc as _bacc
    from concourse import mybir as _mybir
    from concourse.bass_utils import run_bass_kernel_spmd as _run

    nc = _bacc.Bacc("TRN2", target_bir_lowering=False, num_devices=1)
    arrays, args = {}, []
    for name in _INS:
        a = _np.ascontiguousarray(inputs[name])
        a = a.reshape(_SHAPES.get(name, a.shape))
        arrays[f"in_{name}_dram"] = a
        args.append(nc.dram_tensor(f"in_{name}_dram", a.shape, _mybir.dt.from_np(a.dtype), kind="ExternalInput").ap())
    shape = arrays["in_x_dram"].shape
    args.append(nc.dram_tensor("out_0_dram", shape, F32, kind="ExternalOutput").ap())
    gnn_program(nc, *args)
    r = _run(nc, [arrays], core_ids=[0])
    return r.results[0]["out_0_dram"]
```

```python
from contextlib import ExitStack

import concourse.bass as bass
from concourse import mybir

F32 = mybir.dt.float32
F32R = mybir.dt.float32r
I32 = mybir.dt.int32
ALU = mybir.AluOpType
ACT = mybir.ActivationFunctionType

P = 128
D = 256
HEADS = 8
HD = D // HEADS
TILES = 18
GROUP = 3
GROUPS = TILES // GROUP
COLS = GROUP * P
BLOCK_EDGES = TILES * P
FRAME = TILES + 2
ROW = D + HEADS
XBUFS = 4
BATCH = 3
BIG = 1.0e30
STEP = 2.0 ** 90
NO_NODE = 1 << 14
E_MAX = 1.0e9
EPS = 1e-5


class Block_:

    def __init__(self, u, c, blocks, least=0):
        self.u, self.c, self.blocks, self.least = u, c, blocks, least
        self.fixed = isinstance(u, int)

    def shift(self, d):
        return Block_(self.u, self.c + d, self.blocks, self.least)

    @property
    def exists(self):
        if not self.fixed:
            assert self.c >= -3 * self.least
            return True
        return 0 <= 3 * self.u + self.c < self.blocks

    @property
    def is_last(self):
        return self.fixed and 3 * self.u + self.c == self.blocks - 1

    @property
    def buf(self):
        return self.c % 3

    @property
    def index(self):
        return self.u * 3 + self.c

    def count(self, per_block, more=0):
        return self.u * (3 * per_block) + (self.c * per_block + more)

    def uses(self, per_use):
        return self.u * per_use + (self.c // 3 + 1) * per_use

    def positive(self, per_block, more=0):
        return (3 * self.least + self.c) * per_block + more > 0


def behind(i, g, lag):
    s = g - lag
    return i.shift(s // GROUPS), s % GROUPS


def gnn_program(nc, x, src, dst, wi, bi, wj, bj, aw, ab, out):
    n_nodes, n_edges = x.shape[0], src.shape[0]
    blocks = -(-n_nodes // P)
    last_rows = n_nodes - (blocks - 1) * P
    edge_tiles = -(-n_edges // P)
    bounds = blocks + 1
    assert bounds <= P and edge_tiles <= 2048

    s_dram = nc.dram_tensor("sent_rows", [blocks * P, D], F32).ap()
    r_dram = nc.dram_tensor("received_rows", [blocks * P, 2 * D], F32).ap()
    srcp = nc.dram_tensor("src_padded", [n_edges + BLOCK_EDGES], I32).ap()
    dstp = nc.dram_tensor("dst_padded", [edge_tiles * P + BLOCK_EDGES], I32).ap()
    state = nc.dram_tensor("node_states", [(blocks + 1) * P, ROW + HEADS], F32).ap()
    ptr_dram = nc.dram_tensor("row_starts", [bounds], I32).ap()

    ctx = ExitStack()
    with ctx:
        def sb(name, shape, dt=F32):
            return ctx.enter_context(nc.sbuf_tensor(name, shape, dt))

        def sem(name):
            return ctx.enter_context(nc.semaphore(name))

        ident = sb("ident", [P, P])
        node_col = sb("node_col", [P, P])
        w_sb = sb("w_sb", [P, 2, 2 * D])
        bias = sb("bias", [P, 2 * D])
        aw_sb = sb("aw_sb", [P, 1])
        ab_sb = sb("ab_sb", [P, 1])
        score_w = sb("score_w", [P, BATCH, 2, 32])
        zero_row = sb("zero_row", [1, BLOCK_EDGES], I32)
        none_row = sb("none_row", [1, BLOCK_EDGES + P], I32)
        ones_row = sb("ones_row", [1, P])
        firsts_i = sb("firsts_i", [1, edge_tiles], I32)
        firsts = sb("firsts", [1, edge_tiles])
        bound_i = sb("bound_i", [P, 1], I32)
        bound = sb("bound", [P, 1])
        before = sb("before", [P, edge_tiles])
        n_tiles_before = sb("n_tiles_before", [P, 1])
        at_tile = sb("at_tile", [P, 1])
        at_tile_i = sb("at_tile_i", [P, 1], I32)
        edge_row = sb("edge_row", [P, P], I32)
        before_row = sb("before_row", [P, P])
        n_before = sb("n_before", [P, 1])
        starts_i = sb("starts_i", [P, 1], I32)
        starts = sb("starts", [1, bounds], I32)
        xt = sb("xt", [P, XBUFS, D])
        w_part = sb("w_part", [P, 2, 2, 2 * D], F32R)
        xT_part = sb("xT_part", [P, 2, 2, 2, P], F32R)
        sr = sb("sr", [P, XBUFS, 2 * D])
        rhl = sb("rhl", [P, XBUFS, 2, D], F32R)
        src_i = sb("src_i", [P, 3, TILES], I32)
        dst_i = sb("dst_i", [P, 3, TILES], I32)
        s_buf = sb("s_buf", [P, 3, TILES, ROW])
        r_buf = sb("r_buf", [P, 3, 2, D], F32R)
        nbase = sb("nbase", [P, 3])
        dl = sb("dl", [P, 3, TILES])
        dlb = sb("dlb", [P, 3, TILES])
        sel = sb("sel", [P, 3, TILES, P])
        selT = sb("selT", [P, 2, COLS], F32R)
        e_buf = sb("e_buf", [P, 2, 2, COLS])
        h_buf = sb("h_buf", [P, 2, 2, COLS])
        lts = sb("lts", [32 * GROUP, P])
        logit = sb("logit", [P, 3, HEADS, FRAME])
        pen = sb("pen", [P, 3, HEADS * FRAME + 1])
        fwd = sb("fwd", [P, HEADS, FRAME])
        bwd = sb("bwd", [P, HEADS, FRAME])
        dts = sb("dts", [HEADS, 2, P])
        penf = sb("penf", [HEADS, 2, P])
        penb = sb("penb", [HEADS, 2, P])
        tf = sb("tf", [HEADS, P])
        tb = sb("tb", [HEADS, P])
        carry = sb("carry", [HEADS, 2, P])
        top = sb("top", [P, HEADS, TILES])
        diff = sb("diff", [P, HEADS, TILES])
        x_buf = sb("x_buf", [P, 3, D])
        den = sb("den", [P, HEADS])
        rden = sb("rden", [P, HEADS])
        y = sb("y", [P, D])
        yx = sb("yx", [P, D])
        stats = sb("stats", [P, 6])
        mv = sb("mv", [P, 2])
        eps_sb = sb("eps_sb", [P, 1])
        lnv = sb("lnv", [P, 1])
        rs0 = sb("rs0", [P, 1])
        nt = sb("nt", [P, 4])
        rs1 = sb("rs1", [P, 1])
        y_buf = sb("y_buf", [P, 3, D])

        drops = sb("drops", [P, 1])
        unfit = sb("unfit", [1, 4])
        runs = sb("runs", [1, blocks])
        plan = sb("plan", [1, 1], I32)
        aw_row = sb("aw_row", [P, HD])
        g_src = sb("g_src", [P, 1], I32)
        g_dst = sb("g_dst", [P, 1], I32)
        g_node = sb("g_node", [P, 1], I32)
        g_row = sb("g_row", [P, 1], I32)
        g_dstf = sb("g_dstf", [P, 1])
        g_like = sb("g_like", [P, P])
        g_pen = sb("g_pen", [P, P])
        g_logit0 = sb("g_logit0", [P, HEADS])
        g_logit = sb("g_logit", [P, HEADS])
        g_max = sb("g_max", [P, HEADS])
        g_drop = sb("g_drop", [P, HEADS])
        g_args = sb("g_args", [P, 2, HEADS])
        g_fade = sb("g_fade", [P, HEADS])
        s_flat = s_buf[:, :, :, :].rearrange("p a b c -> p (a b c)")
        g_sp = s_flat[:, 0:ROW]
        g_r = s_flat[:, 2 * D:4 * D]
        g_old = s_flat[:, 4 * D:4 * D + ROW + HEADS]
        g_new = s_flat[:, 6 * D:6 * D + ROW + HEADS]
        h_flat = h_buf[:, :, :, :].rearrange("p a b c -> p (a b c)")
        g_z, g_e, g_h = (h_flat[:, n * D:(n + 1) * D] for n in range(3))
        g_masked = e_buf[:, :, :, :].rearrange("p a b c -> p (a b c)")[:, 0:HEADS * P].rearrange(
            "p (h e) -> p h e", e=P)
        sel_flat = sel[:, :, :, :].rearrange("p a b c -> p (a b c)")
        edge_here = sel_flat[:, 0:edge_tiles].bitcast(I32)
        edge_next = sel_flat[:, edge_tiles:2 * edge_tiles].bitcast(I32)
        above = sel_flat[:, 2 * edge_tiles:3 * edge_tiles]

        z_ps = ctx.enter_context(nc.psum_tensor("z_ps", [P, 2, 2, 512], F32))
        pm = ctx.enter_context(nc.psum_tensor("pm", [P, 4, 512], F32))
        selT_ps = pm[:, 0, 0:COLS]
        acc_ps = pm[:, 1, 0:ROW]
        lt_ps = pm[0:32 * GROUP, 2, 0:P]
        misc = pm[:, 3, :]
        edge_first_ps = misc[0:HEADS, 0:2 * P]
        ltt_ps = misc[:, 256:256 + 32 * GROUP]
        carry_ps = misc[:, 384:384 + 2 * HEADS]

        g_logit_ps = z_ps[:, 0]
        g_dst_ps = z_ps[:, 1, 0, 0:P]
        g_sum_ps = z_ps[:, 1, 1, 0:ROW]

        def frame_flat(t, k):
            return t[:, k].rearrange("p h f -> p (h f)")

        s_const = sem("s_const")
        s_pad = sem("s_pad")
        s_first = sem("s_first")
        s_fill = sem("s_fill")
        s_pool_const = sem("s_pool_const")
        s_dve_const = sem("s_dve_const")
        s_firsts_f = sem("s_firsts_f")
        s_bc = sem("s_bc")
        s_at = sem("s_at")
        s_edge_row = sem("s_edge_row")
        s_starts_i = sem("s_starts_i")
        s_starts_d = sem("s_starts_d")
        s_starts = sem("s_starts")
        s_setup = sem("s_setup")
        s_xt = [sem(f"s_xt{a}") for a in range(XBUFS)]
        s_xtr = sem("s_xtr")
        s_whi = sem("s_whi")
        s_wlo = sem("s_wlo")
        s_xhi = sem("s_xhi")
        s_xlo = sem("s_xlo")
        s_proj = sem("s_proj")
        s_sr = sem("s_sr")
        s_rhi = sem("s_rhi")
        s_rlo = sem("s_rlo")
        s_s_out = [sem(f"s_s_out{a}") for a in range(XBUFS)]
        s_r_out = [sem(f"s_r_out{a}") for a in range(XBUFS)]

        src_in = [sem(f"src_in{k}") for k in range(3)]
        dst_in = [sem(f"dst_in{k}") for k in range(3)]
        r_in = [sem(f"r_in{k}") for k in range(3)]
        x_in = [sem(f"x_in{k}") for k in range(3)]
        gathered = [[sem(f"gathered{k}_{g}") for g in range(GROUPS)] for k in range(3)]
        y_out = sem("y_out")
        y_free = sem("y_free")
        prepped = sem("prepped")
        prep_step = sem("prep_step")
        sel_done = sem("sel_done")
        selT_tr = sem("selT_tr")
        selT_done = sem("selT_done")
        z_done = sem("z_done")
        exp_done = sem("exp_done")
        cut_done = sem("cut_done")
        sq_done = sem("sq_done")
        ln_done = sem("ln_done")
        r_done = sem("r_done")
        h_done = sem("h_done")
        score_done = sem("score_done")
        lt_done = sem("lt_done")
        ltt_done = sem("ltt_done")
        logit_done = sem("logit_done")
        ends_tr = sem("ends_tr")
        ends_done = sem("ends_done")
        pens_done = sem("pens_done")
        scan_done = sem("scan_done")
        scan_tr = sem("scan_tr")
        tscan_done = sem("tscan_done")
        carry_done = sem("carry_done")
        carry_tr = sem("carry_tr")
        carry_in = sem("carry_in")
        rescan_done = sem("rescan_done")
        top_done = sem("top_done")
        diff_done = sem("diff_done")
        p_done = sem("p_done")
        msg_done = sem("msg_done")
        out_done = sem("out_done")
        den_done = sem("den_done")
        rden_done = sem("rden_done")
        acc_read = sem("acc_read")
        yx_done = sem("yx_done")
        stats_done = sem("stats_done")
        mv_done = sem("mv_done")
        lnv_done = sem("lnv_done")
        rs0_done = sem("rs0_done")
        newton = sem("newton")
        y_done = sem("y_done")
        s_dst_in = sem("s_dst_in")
        s_drop_step = sem("s_drop_step")
        s_drops = sem("s_drops")
        s_drops_row = sem("s_drops_row")
        s_plan_step = sem("s_plan_step")
        s_plan = sem("s_plan")
        g_first_made = sem("g_first_made")
        g_first_out = sem("g_first_out")
        g_tile_over = sem("g_tile_over")
        g_edges = sem("g_edges")
        g_index = sem("g_index")
        g_gathered = sem("g_gathered")
        g_step = sem("g_step")
        g_z_done = sem("g_z_done")
        g_e_done = sem("g_e_done")
        g_cut_done = sem("g_cut_done")
        g_q_step = sem("g_q_step")
        g_r_done = sem("g_r_done")
        g_dst_all = sem("g_dst_all")
        g_logit_done = sem("g_logit_done")
        g_logit_all = sem("g_logit_all")
        g_args_done = sem("g_args_done")
        g_p_done = sem("g_p_done")
        g_msg_done = sem("g_msg_done")
        g_sum_done = sem("g_sum_done")
        g_new_done = sem("g_new_done")
        g_scattered = sem("g_scattered")
        g_rows_in = sem("g_rows_in")
        sp_passed = sem("sp_passed")
        pool_passed = sem("pool_passed")
        dve_passed = sem("dve_passed")

        block = ctx.enter_context(nc.Block())

        def iterations(eng, body, first=-1, last=None, peeled=1):
            last = blocks + 3 if last is None else last
            turns = max((blocks - 2) // 3, peeled)
            for c in range(first, min(3 * peeled, last + 1)):
                body(Block_(0, c, blocks))
            if turns > peeled:
                with eng.Fori(peeled, turns) as u:
                    for c in range(3):
                        body(Block_(u, c, blocks, peeled))
            for c in range(3 * turns, last + 1):
                body(Block_(0, c, blocks))

        def projected_tiles(eng, body):
            turns = (blocks - 1) // XBUFS
            assert turns >= 2
            for v in range(2):
                for a in range(XBUFS):
                    body(v, a)
            if turns > 2:
                with eng.Fori(2, turns) as v:
                    for a in range(XBUFS):
                        body(v, a)
            for a in range(blocks - XBUFS * turns):
                body(turns, a)

        def past(v, a, n):
            return (XBUFS * v + a if isinstance(v, int) else 2 * XBUFS + a) >= n

        def stored(a):
            return 16 * -(-(blocks - a) // XBUFS)

        @block.sync
        def _(sp):
            sp.dma_start(firsts_i[0:1, :], dst.rearrange("(a e) -> a e", a=1)[:, 0:n_edges:P],
                         allow_slow_non_contiguous=True).then_inc(s_first, 16)
            for k in range(2):
                sp.dma_start(w_sb[:, k, 0:D], wi[k * P:(k + 1) * P, :]).then_inc(s_const, 16)
                sp.dma_start(w_sb[:, k, D:2 * D], wj[k * P:(k + 1) * P, :]).then_inc(s_const, 16)
            sp.dma_start(bias[:, 0:D], bi.broadcast_to([P, D])).then_inc(s_const, 16)
            sp.dma_start(bias[:, D:2 * D], bj.broadcast_to([P, D])).then_inc(s_const, 16)
            for g in range(P // HD):
                sp.dma_start(aw_sb[g * HD:(g + 1) * HD, :], aw).then_inc(s_const, 16)
            sp.dma_start(ab_sb[:, :], ab.broadcast_to([P, 1])).then_inc(s_const, 16)
            sp.dma_start(aw_row[:, :], aw.rearrange("c a -> a c").broadcast_to([P, HD])).then_inc(s_const, 16)
            sp.dma_start(srcp[0:n_edges], src).then_inc(s_pad, 16)
            sp.dma_start(dstp[0:n_edges], dst).then_inc(s_pad, 16)
            sp.wait_ge(s_fill, 2)
            sp.dma_start(srcp[n_edges:n_edges + BLOCK_EDGES].rearrange("(a e) -> a e", a=1),
                         zero_row[:, :]).then_inc(s_pad, 16)
            tail = edge_tiles * P + BLOCK_EDGES - n_edges
            sp.dma_start(dstp[n_edges:n_edges + tail].rearrange("(a e) -> a e", a=1),
                         none_row[:, 0:tail]).then_inc(s_pad, 16)

            def load_rows(v, a):
                rows = last_rows if isinstance(v, int) and XBUFS * v + a == blocks - 1 else P
                if past(v, a, XBUFS):
                    sp.wait_ge(s_xtr, v * XBUFS + (a - XBUFS + 1))
                    sp.sem_inc(sp_passed, 1)
                sp.dma_start(xt[0:rows, a, :], x[bass.ds(v * (XBUFS * P) + a * P, rows), :]).then_inc(s_xt[a], 16)

            def store_r(v, a):
                sp.wait_ge(s_rlo, v * XBUFS + (a + 1))
                sp.sem_inc(sp_passed, 1)
                sp.dma_start(r_dram[bass.ds(v * (XBUFS * P) + a * P, P), :],
                             rhl[:, a].bitcast(F32).rearrange("p a b -> p (a b)")).then_inc(s_r_out[a], 16)

            def project(v, a):
                load_rows(v, a)
                if past(v, a, XBUFS):
                    store_r(v - 1, a)

            projected_tiles(sp, project)
            last_stores = [(t // XBUFS, t % XBUFS) for t in range(blocks - XBUFS, blocks)]
            sp.wait_ge(s_starts_i, 1)
            sp.dma_start(ptr_dram.rearrange("(b a) -> b a", a=1), starts_i[0:bounds, :]).then_inc(s_starts_d, 16)
            for v, a in last_stores[:2]:
                store_r(v, a)
            sp.wait_ge(s_starts_d, 16)
            sp.dma_start(starts[0:1, :], ptr_dram.rearrange("(a b) -> a b", a=1)).then_inc(s_starts, 16)
            for v, a in last_stores[2:]:
                store_r(v, a)
            sp.wait_ge(s_starts, 16)
            sp.wait_ge(s_pad, 64)
            for a in range(XBUFS):
                sp.wait_ge(s_r_out[a], stored(a) - 16)
            def blocks_path():
                sp.sem_inc(y_free, 3)

                def load(j):
                    old = j.shift(-3)
                    start = sp.value_load(starts[0:1, bass.ds(j.index, 1)], min_val=0, max_val=n_edges)
                    first_row = j.count(P)
                    if old.exists:
                        for g in range(GROUPS):
                            sp.wait_ge(gathered[old.buf][g], old.uses(16 * GROUP))
                        sp.sem_inc(sp_passed, 1)
                        sp.wait_ge(prepped, old.count(1, 1))
                        sp.sem_inc(sp_passed, 1)
                        sp.wait_ge(z_done, old.count(GROUPS, GROUPS))
                        sp.sem_inc(sp_passed, 1)
                    k = j.buf
                    sp.dma_start(src_i[:, k, :], srcp[bass.ds(start, BLOCK_EDGES)].rearrange(
                        "(p j) -> p j", j=TILES)).then_inc(src_in[k], 16)
                    sp.dma_start(dst_i[:, k, :], dstp[bass.ds(start, BLOCK_EDGES)].rearrange(
                        "(p j) -> p j", j=TILES)).then_inc(dst_in[k], 16)
                    sp.dma_start(r_buf[:, k].bitcast(F32).rearrange("p a b -> p (a b)"),
                                 r_dram[bass.ds(first_row, P), :]).then_inc(r_in[k], 16)

                def load_x(i):
                    old, k = i.shift(-3), i.buf
                    rows = last_rows if i.is_last else P
                    first_row = i.count(P)
                    if old.exists:
                        sp.wait_ge(yx_done, old.count(1, 1))
                        sp.sem_inc(sp_passed, 1)
                    sp.dma_start(x_buf[0:rows, k, :], x[bass.ds(first_row, rows), :]).then_inc(x_in[k], 16)

                def store_y(b):
                    rows = last_rows if b.is_last else P
                    first_row = b.count(P)
                    sp.wait_ge(y_done, b.count(1, 1))
                    sp.sem_inc(sp_passed, 1)
                    sp.dma_start(out[bass.ds(first_row, rows), :], y_buf[0:rows, b.buf, :]).then_inc(y_out, 16)
                    sp.wait_ge(y_out, b.count(16, 16))
                    sp.sem_inc(y_free, 1)

                load(Block_(0, 0, blocks))
                for a in range(XBUFS):
                    sp.wait_ge(s_r_out[a], stored(a))

                def body(i):
                    if i.shift(2).exists:
                        load(i.shift(2))
                    if i.exists:
                        load_x(i)
                    if i.shift(-4).exists:
                        store_y(i.shift(-4))

                iterations(sp, body, last=blocks + 4, peeled=2)

            def tiles_path():
                for a in range(XBUFS):
                    sp.wait_ge(s_r_out[a], stored(a))
                sp.wait_ge(g_first_made, 1)
                with sp.Fori(0, blocks + 1) as b:
                    sp.dma_start(state[bass.ds(b * P, P), :], g_old[:, :]).then_inc(g_first_out, 16)
                with sp.Fori(0, edge_tiles) as t:
                    sp.wait_ge(g_tile_over, t + 1)
                    sp.sem_inc(sp_passed, 1)
                    sp.dma_start(g_src[:, :], srcp[bass.ds(t * P, P)].rearrange("(p a) -> p a", a=1)).then_inc(g_edges, 16)
                    sp.dma_start(g_dst[:, :], dstp[bass.ds(t * P, P)].rearrange("(p a) -> p a", a=1)).then_inc(g_edges, 16)
                sp.wait_ge(g_tile_over, edge_tiles + 1)

                def finish(b, rows):
                    sp.dma_start(g_old[:, :], state[bass.ds(b * P, P), :]).then_inc(g_rows_in, 16)
                    sp.dma_start(x_buf[0:rows, 0, :], x[bass.ds(b * P, rows), :]).then_inc(g_rows_in, 16)
                    sp.wait_ge(y_done, b + 1)
                    sp.sem_inc(sp_passed, 1)
                    sp.dma_start(out[bass.ds(b * P, rows), :], y_buf[0:rows, 0, :]).then_inc(y_out, 16)
                    sp.wait_ge(y_out, b * 16 + 16)
                    sp.sem_inc(sp_passed, 1)

                with sp.Fori(0, blocks - 1) as b:
                    finish(b, P)
                finish(blocks - 1, last_rows)

            sp.wait_ge(s_plan, 1)
            plan_now = sp.value_load(plan[0:1, 0:1], min_val=0, max_val=1)
            with sp.If(plan_now == 0):
                blocks_path()
            with sp.Else():
                tiles_path()

        @block.gpsimd
        def _(pool):
            pool.memset(zero_row[:, :], 0).then_inc(s_fill, 1)
            pool.memset(none_row[:, :], NO_NODE).then_inc(s_fill, 1)
            pool.memset(ones_row[:, :], 1.0).then_inc(s_pool_const, 1)
            pool.memset(ident[:, :], 0.0).then_inc(s_pool_const, 1)
            pool.iota(node_col[:, :], pattern=[[1, P]], base=0, channel_multiplier=0,
                      allow_small_or_imprecise_dtypes=True).then_inc(s_pool_const, 1)
            pool.iota(bound_i[:, :], pattern=[[0, 1]], base=0, channel_multiplier=P).then_inc(s_pool_const, 1)
            pool.wait_ge(s_pool_const, 4)
            pool.affine_select(out=ident[:, :], in_=ident[:, :], compare_op=ALU.not_equal, fill=1.0,
                               base=0, pattern=[[-1, P]], channel_multiplier=1).then_inc(s_pool_const, 1)
            pool.wait_ge(s_pad, 64)
            for side, first in ((edge_here, 0), (edge_next, 1)):
                pool.dma_start(side, dstp[first:first + P * edge_tiles].rearrange(
                    "(p e) -> p e", e=edge_tiles)).then_inc(s_dst_in, 16)
            pool.wait_ge(s_at, 1)
            pool.indirect_dma_start(
                out=edge_row[0:bounds, :], out_offset=None,
                in_=dstp[0:edge_tiles * P].rearrange("(t e) -> t e", e=P),
                in_offset=bass.IndirectOffsetOnAxis(ap=at_tile_i[0:bounds, 0:1], axis=0),
            ).then_inc(s_edge_row, 16)

            def store_s(v, a):
                pool.wait_ge(s_sr, v * XBUFS + (a + 1))
                pool.sem_inc(pool_passed, 1)
                pool.dma_start(s_dram[bass.ds(v * (XBUFS * P) + a * P, P), :],
                               sr[:, a, 0:D]).then_inc(s_s_out[a], 16)

            projected_tiles(pool, store_s)
            for a in range(XBUFS):
                pool.wait_ge(s_s_out[a], stored(a))

            def refine(before):
                def step(n):
                    pool.wait_ge(newton, before * 5 + n)
                    pool.sem_inc(pool_passed, 1)

                pool.wait_ge(rs0_done, before + 1)
                pool.sem_inc(pool_passed, 1)
                pool.tensor_scalar(nt[:, 0:1], mv[:, 1:2], EPS, None, ALU.add).then_inc(newton, 1)
                step(1)
                pool.tensor_tensor(nt[:, 1:2], nt[:, 0:1], rs0[:, :], ALU.mult).then_inc(newton, 1)
                step(2)
                pool.tensor_tensor(nt[:, 2:3], nt[:, 1:2], rs0[:, :], ALU.mult).then_inc(newton, 1)
                step(3)
                pool.tensor_scalar(nt[:, 3:4], nt[:, 2:3], -0.5, 1.5, ALU.mult, ALU.add).then_inc(newton, 1)
                step(4)
                pool.tensor_tensor(rs1[:, :], nt[:, 3:4], rs0[:, :], ALU.mult).then_inc(newton, 1)

            def blocks_path():
                def gather(j, g):
                    k, old = j.buf, j.shift(-3)
                    if old.exists:
                        pool.wait_ge(out_done, old.count(GROUPS, g + 1))
                        pool.sem_inc(pool_passed, 1)
                    for t in range(GROUP * g, GROUP * (g + 1)):
                        pool.indirect_dma_start(
                            out=s_buf[:, k, t, 0:D], out_offset=None, in_=s_dram,
                            in_offset=bass.IndirectOffsetOnAxis(ap=src_i[:, k, t:t + 1], axis=0),
                        ).then_inc(gathered[k][g], 16)

                def penalties(b):
                    pool.wait_ge(ends_done, b.count(1, 1))
                    pool.sem_inc(pool_passed, 1)
                    if b.positive(1):
                        pool.wait_ge(carry_done, b.count(1))
                        pool.sem_inc(pool_passed, 1)
                    pool.tensor_tensor(penf[:, :, 1:P], dts[:, 1:2, 0:P - 1].broadcast_to([HEADS, 2, P - 1]),
                                       dts[:, ::-1, 1:P], ALU.subtract)
                    pool.tensor_tensor(penb[:, :, 0:P - 1], dts[:, :, 0:P - 1],
                                       dts[:, 0:1, 1:P].broadcast_to([HEADS, 2, P - 1]),
                                       ALU.subtract).then_inc(pens_done, 1)

                def body(j):
                    if j.exists:
                        pool.wait_ge(src_in[j.buf], j.uses(16))
                        pool.sem_inc(pool_passed, 1)
                    for g in range(GROUPS):
                        if j.exists:
                            gather(j, g)
                        if g == 1 and j.shift(-2).exists:
                            penalties(j.shift(-2))
                        b = j.shift(-4)
                        if g == 3 and b.exists:
                            refine(b.count(1))

                iterations(pool, body, first=0, last=blocks + 3, peeled=2)

            def tiles_path():
                pool.wait_ge(g_first_out, 16 * (blocks + 1))
                pool.sem_inc(g_tile_over, 1)
                with pool.Fori(0, edge_tiles) as t:
                    pool.wait_ge(g_index, t + 1)
                    pool.sem_inc(pool_passed, 1)
                    for rows, table, index in ((g_sp[:, 0:D], s_dram, g_src), (g_r[:, :], r_dram, g_node),
                                               (g_old[:, :], state, g_row)):
                        pool.indirect_dma_start(
                            out=rows, out_offset=None, in_=table,
                            in_offset=bass.IndirectOffsetOnAxis(ap=index[:, 0:1], axis=0),
                        ).then_inc(g_gathered, 16)
                    pool.wait_ge(g_new_done, t + 1)
                    pool.sem_inc(pool_passed, 1)
                    pool.indirect_dma_start(
                        out=state, out_offset=bass.IndirectOffsetOnAxis(ap=g_row[:, 0:1], axis=0),
                        in_=g_new[:, :], in_offset=None,
                    ).then_inc(g_scattered, 16)
                    pool.wait_ge(g_scattered, t * 16 + 16)
                    pool.sem_inc(g_tile_over, 1)
                with pool.Fori(0, blocks) as b:
                    refine(b)

            pool.wait_ge(s_plan, 1)
            plan_now = pool.value_load(plan[0:1, 0:1], min_val=0, max_val=1)
            with pool.If(plan_now == 0):
                blocks_path()
            with pool.Else():
                tiles_path()

        @block.scalar
        def _(act):
            act.preload_act_table_set("natural_log_exp_and_others")

            act.wait_ge(s_const, 16 * (8 + P // HD))
            act.activation(w_part[:, 0], w_sb[:, :, :], ACT.Copy).then_inc(s_whi, 1)

            def project(v, a):
                act.wait_ge(s_xtr, v * XBUFS + (a + 1))
                if past(v, a, 2):
                    act.wait_ge(s_proj, v * XBUFS + (a - 1))
                act.activation(xT_part[:, a % 2, 0].rearrange("p k n -> p (k n)"), z_ps[:, a % 2, 0, 0:2 * P],
                               ACT.Copy).then_inc(s_xhi, 1)
                if past(v, a, 1):
                    split_hi(v, a - 1)

            def split_hi(v, a):
                act.wait_ge(s_sr, v * XBUFS + (a + 1))
                if past(v, a, XBUFS):
                    act.wait_ge(s_r_out[a % XBUFS], (v + a // XBUFS) * 16)
                act.activation(rhl[:, a % XBUFS, 0, :], sr[:, a % XBUFS, D:2 * D], ACT.Copy).then_inc(s_rhi, 1)

            projected_tiles(act, project)
            split_hi(0, blocks - 1)

            def blocks_path():
                def slot(i, g):
                    par = g % 2
                    if i.exists:
                        act.wait_ge(z_done, i.count(GROUPS, g + 1))
                        act.activation(e_buf[:, par], z_ps[:, par, :, 0:COLS], ACT.Exp).then_inc(exp_done, 1)
                    j, h = behind(i, g, 1)
                    if j.exists:
                        act.wait_ge(ln_done, j.count(GROUPS, h + 1))
                        for hf in range(2):
                            act.activation(e_buf[:, 1 - par, hf], e_buf[:, 1 - par, hf], ACT.Exp,
                                           scale=-1.0).then_inc(r_done, 1)
                    if i.exists:
                        act.wait_ge(cut_done, i.count(GROUPS, g + 1))
                        act.activation(e_buf[:, par], e_buf[:, par], ACT.Square, bias=1.0).then_inc(sq_done, 1)
                    b = i.shift(-1)
                    if g == GROUPS - 1 and b.exists:
                        act.wait_ge(diff_done, b.count(1, 1))
                        act.activation(s_buf[:, b.buf, :, D:ROW].rearrange("p j h -> p h j"), diff[:, :, :],
                                       ACT.Exp).then_inc(p_done, 1)
                    j, h = behind(i, g, -2)
                    if j.exists:
                        act.wait_ge(selT_tr, j.count(GROUPS, h + 1))
                        act.activation(selT[:, par, :], selT_ps, ACT.Copy).then_inc(selT_done, 1)
                    j, h = behind(i, g, 3)
                    if j.exists and h % BATCH == BATCH - 1:
                        w = h // BATCH
                        act.wait_ge(ltt_done, j.count(2, w + 1))
                        first = 1 + w * BATCH * GROUP
                        act.activation(
                            logit[:, j.buf, :, first:first + BATCH * GROUP].rearrange("p h (v t) -> p t v h", t=GROUP),
                            ltt_ps.rearrange("p (t q) -> p t q", t=GROUP)[:, :, 0:BATCH * HEADS].rearrange(
                                "p t (v h) -> p t v h", h=HEADS),
                            ACT.Identity, bias=ab_sb[:, 0:1]).then_inc(logit_done, 1)
                    b = i.shift(-1)
                    if b.exists and g == 1:
                        act.wait_ge(ends_tr, b.count(1, 1))
                        if b.positive(1):
                            act.wait_ge(pens_done, b.count(1))
                        act.activation(dts[:, :, :].rearrange("h a p -> h (a p)"), edge_first_ps,
                                       ACT.Copy).then_inc(ends_done, 1)
                    j, h = behind(i, g, 2)
                    if j.exists and h % BATCH == BATCH - 1:
                        w = h // BATCH
                        act.wait_ge(score_done, j.count(GROUPS, h + 1))
                        if j.positive(2, w):
                            act.wait_ge(ltt_done, j.count(2, w))
                        act.activation(lts[:, :], lt_ps, ACT.Copy).then_inc(lt_done, 1)
                    b = i.shift(-3)
                    if g == 2 and b.exists:
                        act.wait_ge(mv_done, b.count(1, 1))
                        act.activation(lnv[:, :], mv[:, 1:2], ACT.Ln, bias=eps_sb[:, 0:1]).then_inc(lnv_done, 1)
                    if i.exists:
                        act.wait_ge(sq_done, i.count(GROUPS, g + 1))
                        act.activation(e_buf[:, par], e_buf[:, par], ACT.Ln, bias=1.0).then_inc(ln_done, 1)
                    if g == 2 and b.exists:
                        act.wait_ge(lnv_done, b.count(1, 1))
                        act.activation(rs0[:, :], lnv[:, :], ACT.Exp, scale=-0.5).then_inc(rs0_done, 1)

                def body(i):
                    for g in range(GROUPS):
                        slot(i, g)

                iterations(act, body)

            def tiles_path():
                with act.Fori(0, edge_tiles) as t:
                    act.wait_ge(g_z_done, t + 1)
                    act.activation(g_e, g_z, ACT.Exp).then_inc(g_e_done, 1)
                    act.wait_ge(g_cut_done, t + 1)
                    act.activation(g_e, g_e, ACT.Square, bias=1.0).then_inc(g_q_step, 1)
                    act.wait_ge(g_q_step, t * 2 + 1)
                    act.activation(g_e, g_e, ACT.Ln, bias=1.0).then_inc(g_q_step, 1)
                    act.wait_ge(g_q_step, t * 2 + 2)
                    act.activation(g_e, g_e, ACT.Exp, scale=-1.0).then_inc(g_r_done, 1)
                    act.wait_ge(g_args_done, t + 1)
                    act.activation(g_sp[:, D:ROW], g_args[:, 0, :], ACT.Exp)
                    act.activation(g_fade[:, :], g_args[:, 1, :], ACT.Exp).then_inc(g_p_done, 1)

                def finish(b):
                    act.wait_ge(mv_done, b + 1)
                    act.activation(lnv[:, :], mv[:, 1:2], ACT.Ln, bias=eps_sb[:, 0:1]).then_inc(lnv_done, 1)
                    act.wait_ge(lnv_done, b + 1)
                    act.activation(rs0[:, :], lnv[:, :], ACT.Exp, scale=-0.5).then_inc(rs0_done, 1)

                with act.Fori(0, blocks) as b:
                    finish(b)

            act.wait_ge(s_plan, 1)
            plan_now = act.value_load(plan[0:1, 0:1], min_val=0, max_val=1)
            with act.If(plan_now == 0):
                blocks_path()
            with act.Else():
                tiles_path()

        @block.tensor
        def _(pe):
            pe.wait_ge(s_pool_const, 5)
            pe.wait_ge(s_firsts_f, 1)
            for c in range(0, edge_tiles, 512):
                m = min(512, edge_tiles - c)
                last = pe.matmul(pm[:, c // 512, 0:m], ones_row[0:1, :], firsts[0:1, c:c + m],
                                 start=True, stop=True)
            last.then_inc(s_bc, 1)

            def product(v, a):
                pe.wait_ge(s_xlo, v * XBUFS + (a + 1))
                if past(v, a, 2):
                    pe.wait_ge(s_sr, v * XBUFS + (a - 1))
                terms = [(xp, wp, k) for xp, wp in ((0, 0), (0, 1), (1, 0)) for k in range(2)]
                for n, (xp, wp, k) in enumerate(terms):
                    last = pe.matmul(z_ps[:, a % 2, 1, :], xT_part[:, a % 2, xp, k, :], w_part[:, wp, k, :],
                                     start=n == 0, stop=n == len(terms) - 1)
                last.then_inc(s_proj, 1)

            def project(v, a):
                pe.wait_ge(s_xt[a], v * 16 + 16)
                if past(v, a, 2):
                    pe.wait_ge(s_xlo, v * XBUFS + (a - 1))
                for k in range(2):
                    last = pe.transpose(z_ps[:, a % 2, 0, k * P:(k + 1) * P], xt[:, a, k * P:(k + 1) * P], ident[:, :])
                last.then_inc(s_xtr, 1)
                if past(v, a, 1):
                    product(v, a - 1)

            pe.wait_ge(s_wlo, 1)
            projected_tiles(pe, project)
            product(0, blocks - 1)
            pe.wait_ge(s_setup, 1)
            pe.wait_ge(s_sr, blocks)
            pe.wait_ge(s_drops, 1)
            pe.matmul(pm[0:1, 3, 0:P], drops[:, 0:1], ident[:, :], start=True, stop=True).then_inc(s_drops_row, 1)

            def blocks_path():
                def slot(i, g):
                    par = g % 2
                    if i.exists:
                        k = i.buf
                        pe.wait_ge(selT_done, i.count(GROUPS, g + 1))
                        if g == 0:
                            pe.wait_ge(r_in[k], i.uses(16))
                        pe.wait_ge(gathered[k][g], i.uses(16 * GROUP))
                        for hf in range(2):
                            if i.positive(2 * GROUPS, 2 * (g - 2) + hf + 1):
                                pe.wait_ge(h_done, i.count(2 * GROUPS, 2 * (g - 2) + hf + 1))
                            f = slice(hf * P, (hf + 1) * P)
                            for t in range(GROUP):
                                pe.matmul(z_ps[:, par, hf, t * P:(t + 1) * P], s_buf[:, k, GROUP * g + t, f],
                                          ident[:, :], is_transpose=True, start=t == 0, stop=False)
                            for part in range(2):
                                last = pe.matmul(z_ps[:, par, hf, 0:COLS], r_buf[:, k, part, f], selT[:, par, :],
                                                 start=False, stop=part == 1)
                        last.then_inc(z_done, 1)
                    j, h = behind(i, g, 2)
                    if j.exists:
                        w, v = h // BATCH, h % BATCH
                        pe.wait_ge(h_done, j.count(2 * GROUPS, 2 * h + 2))
                        if v == 0 and j.positive(2, w):
                            pe.wait_ge(lt_done, j.count(2, w))
                        for hf in range(2):
                            for t in range(GROUP):
                                last = pe.matmul(lt_ps[32 * t:32 * t + 32, :], score_w[:, v, hf, :],
                                                 h_buf[:, par, hf, t * P:(t + 1) * P],
                                                 start=v == 0 and hf == 0, stop=v == BATCH - 1 and hf == 1,
                                                 tile_position=(0, 32 * t))
                        last.then_inc(score_done, 1)
                    j, h = behind(i, g, -2)
                    if j.exists:
                        pe.wait_ge(sel_done, j.count(GROUPS, h + 1))
                        if j.positive(GROUPS, h):
                            pe.wait_ge(selT_done, j.count(GROUPS, h))
                        for t in range(GROUP):
                            last = pe.transpose(selT_ps[:, t * P:(t + 1) * P], sel[:, j.buf, GROUP * h + t, :],
                                                ident[:, :])
                        last.then_inc(selT_tr, 1)
                    j, h = behind(i, g, 3)
                    if j.exists and h % BATCH == BATCH - 1:
                        w = h // BATCH
                        pe.wait_ge(lt_done, j.count(2, w + 1))
                        if w == 1:
                            pe.wait_ge(ends_done, j.count(1, 1))
                        elif j.positive(1):
                            pe.wait_ge(carry_in, j.count(1))
                        pe.transpose(ltt_ps, lts[:, :], ident[0:32 * GROUP, 0:32 * GROUP]).then_inc(ltt_done, 1)
                    b = i.shift(-1)
                    if b.exists and g == 0:
                        pe.wait_ge(prepped, b.count(1, 1))
                        pe.wait_ge(logit_done, b.count(2, 1))
                        for n, j_ in enumerate((0, TILES - 1)):
                            last = pe.transpose(edge_first_ps[:, n * P:(n + 1) * P],
                                                dlb[:, b.buf, j_:j_ + 1].broadcast_to([P, HEADS]), ident[:, :])
                        last.then_inc(ends_tr, 1)
                    if b.exists and g == 3:
                        pe.wait_ge(scan_done, b.count(1, 1))
                        pe.transpose(edge_first_ps[:, 0:P], fwd[:, :, TILES], ident[:, :])
                        pe.transpose(edge_first_ps[:, P:2 * P], bwd[:, :, 1], ident[:, :]).then_inc(scan_tr, 1)
                    if b.exists and g == 4:
                        pe.wait_ge(carry_done, b.count(1, 1))
                        for n in range(2):
                            last = pe.matmul(carry_ps[:, n * HEADS:(n + 1) * HEADS], carry[:, n, :],
                                             ident[0:HEADS, 0:HEADS], start=True, stop=True)
                        last.then_inc(carry_tr, 1)
                    j, h = behind(i, g, 12)
                    if j.exists:
                        pe.wait_ge(msg_done, j.count(GROUPS, h + 1))
                        if h == 0 and j.positive(1):
                            pe.wait_ge(acc_read, j.count(1))
                        for t in range(GROUP * h, GROUP * (h + 1)):
                            last = pe.matmul(acc_ps, sel[:, j.buf, t, :], s_buf[:, j.buf, t, :],
                                             start=t == 0, stop=t == TILES - 1)
                        last.then_inc(out_done, 1)

                def body(i):
                    for g in range(GROUPS):
                        slot(i, g)

                iterations(pe, body)

            def tiles_path():
                with pe.Fori(0, edge_tiles) as t:
                    pe.wait_ge(g_index, t + 1)
                    pe.matmul(g_dst_ps, g_dstf[:, 0:1].broadcast_to([P, P]), ident[:, :],
                              start=True, stop=True).then_inc(g_dst_all, 1)
                    pe.wait_ge(g_logit_done, t + 1)
                    for h in range(HEADS):
                        last = pe.matmul(g_logit_ps[:, h // 4, (h % 4) * P:(h % 4 + 1) * P],
                                         g_logit[:, h:h + 1].broadcast_to([P, P]), ident[:, :], start=True, stop=True)
                    last.then_inc(g_logit_all, 1)
                    pe.wait_ge(g_msg_done, t + 1)
                    pe.matmul(g_sum_ps, g_like[:, :], g_sp[:, :], start=True, stop=True).then_inc(g_sum_done, 1)

            pe.wait_ge(s_plan, 1)
            plan_now = pe.value_load(plan[0:1, 0:1], min_val=0, max_val=1)
            with pe.If(plan_now == 0):
                blocks_path()
            with pe.Else():
                tiles_path()

        @block.vector
        def _(dve):
            dve.memset(score_w[:, :, :, :], 0.0).then_inc(s_dve_const, 1)
            dve.memset(pen[:, :, :], 0.0).then_inc(s_dve_const, 1)
            dve.memset(eps_sb[:, :], EPS).then_inc(s_dve_const, 1)
            dve.memset(carry[:, :, :], -BIG).then_inc(s_dve_const, 1)
            dve.memset(penf[:, :, :], 0.0).then_inc(s_dve_const, 1)
            dve.memset(penb[:, :, :], 0.0).then_inc(s_dve_const, 1)
            for k in range(3):
                dve.memset(nbase[:, k:k + 1], -float(P * k)).then_inc(s_dve_const, 1)
            dve.wait_ge(s_dve_const, 9)
            for k in range(3):
                last = dve.memset(pen[:, k, 0:HEADS * FRAME + 1:FRAME], -BIG)
            last.then_inc(s_dve_const, 1)

            dve.wait_ge(s_first, 16)
            dve.tensor_copy(firsts[0:1, :], firsts_i[0:1, :]).then_inc(s_firsts_f, 1)
            dve.wait_ge(s_pool_const, 5)
            dve.tensor_copy(bound[:, :], bound_i[:, :]).then_inc(s_firsts_f, 1)
            dve.wait_ge(s_bc, 1)
            dve.wait_ge(s_firsts_f, 2)
            dve.tensor_scalar(before[:, :], pm[:, :, :].rearrange("p a b -> p (a b)")[:, 0:edge_tiles],
                              bound[:, 0:1], None, ALU.is_lt).then_inc(s_firsts_f, 1)
            dve.wait_ge(s_firsts_f, 3)
            dve.reduce_sum(n_tiles_before[:, :], before[:, :], mybir.AxisListType.X).then_inc(s_firsts_f, 1)
            dve.wait_ge(s_firsts_f, 4)
            dve.tensor_scalar(at_tile[:, :], n_tiles_before[:, :], -1.0, 0.0, ALU.add, ALU.max).then_inc(s_firsts_f, 1)
            dve.wait_ge(s_firsts_f, 5)
            dve.tensor_copy(at_tile_i[:, :], at_tile[:, :]).then_inc(s_at, 1)

            def finish_setup():
                dve.wait_ge(s_dst_in, 32)
                dve.tensor_tensor(above, edge_here, edge_next, ALU.is_gt).then_inc(s_drop_step, 1)
                dve.wait_ge(s_drop_step, 1)
                dve.reduce_max(drops[:, :], above, mybir.AxisListType.X).then_inc(s_drops, 1)

                dve.wait_ge(s_edge_row, 16)
                dve.tensor_scalar(before_row[0:bounds, :], edge_row[0:bounds, :], bound[0:bounds, 0:1], None,
                                  ALU.is_lt).then_inc(s_firsts_f, 1)
                dve.wait_ge(s_firsts_f, 6)
                dve.reduce_sum(n_before[0:bounds, :], before_row[0:bounds, :], mybir.AxisListType.X).then_inc(s_firsts_f, 1)
                dve.wait_ge(s_firsts_f, 7)
                dve.scalar_tensor_tensor(starts_i[0:bounds, :], at_tile[0:bounds, :], float(P), n_before[0:bounds, :],
                                         ALU.mult, ALU.add).then_inc(s_starts_i, 1)
                dve.wait_ge(s_const, 16 * (8 + P // HD))
                for hf in range(2):
                    for q in range(P // HD):
                        for v in range(BATCH):
                            at = v * HEADS + hf * (P // HD) + q
                            last = dve.tensor_scalar(score_w[q * HD:(q + 1) * HD, v, hf, at:at + 1],
                                                     aw_sb[q * HD:(q + 1) * HD, :], -2.0, None, ALU.mult)
                last.then_inc(s_setup, 1)

            dve.wait_ge(s_const, 16 * (8 + P // HD))
            dve.wait_ge(s_whi, 1)
            dve.tensor_tensor(w_part[:, 1], w_sb[:, :, :], w_part[:, 0].bitcast(F32), ALU.subtract).then_inc(s_wlo, 1)

            def project(v, a):
                dve.wait_ge(s_xhi, v * XBUFS + (a + 1))
                dve.tensor_tensor(xT_part[:, a % 2, 1].rearrange("p k n -> p (k n)"), z_ps[:, a % 2, 0, 0:2 * P],
                                  xT_part[:, a % 2, 0].rearrange("p k n -> p (k n)").bitcast(F32),
                                  ALU.subtract).then_inc(s_xlo, 1)
                if past(v, a, 2):
                    split_lo(v, a - 2)
                if past(v, a, 1):
                    add_bias(v, a - 1)
                if isinstance(v, int) and (v, a) == (1, 0):
                    finish_setup()

            def add_bias(v, a):
                dve.wait_ge(s_proj, v * XBUFS + (a + 1))
                if past(v, a, XBUFS):
                    dve.wait_ge(s_s_out[a % XBUFS], (v + a // XBUFS) * 16)
                dve.tensor_tensor(sr[:, a % XBUFS, :], z_ps[:, a % 2, 1, :], bias[:, :], ALU.add).then_inc(s_sr, 1)

            def split_lo(v, a):
                dve.wait_ge(s_rhi, v * XBUFS + (a + 1))
                dve.tensor_tensor(rhl[:, a % XBUFS, 1, :], sr[:, a % XBUFS, D:2 * D],
                                  rhl[:, a % XBUFS, 0, :].bitcast(F32), ALU.subtract).then_inc(s_rlo, 1)

            projected_tiles(dve, project)
            split_lo(0, blocks - 2)
            add_bias(0, blocks - 1)
            split_lo(0, blocks - 1)

            def scale_rows(k, before):
                dve.wait_ge(newton, before * 5 + 5)
                dve.tensor_scalar(y_buf[:, k, :], yx[:, :], mv[:, 0:1], rs1[:, 0:1], ALU.subtract,
                                  ALU.mult).then_inc(y_done, 1)

            def blocks_path():
                def prep(j, part):
                    k = j.buf
                    if part == 0:
                        dve.wait_ge(dst_in[k], j.uses(16))
                        dve.tensor_scalar(dl[:, k, :], dst_i[:, k, :], nbase[:, k:k + 1], None,
                                          ALU.add).then_inc(prep_step, 1)
                        dve.memset(logit[:, k, :, 0:FRAME:FRAME - 1], -BIG)
                    elif part == 1:
                        dve.wait_ge(prep_step, j.count(3, 1))
                        dve.tensor_scalar(dlb[:, k, :], dl[:, k, :], STEP, None, ALU.mult).then_inc(prep_step, 1)
                        dve.tensor_scalar(nbase[:, k:k + 1], nbase[:, k:k + 1], -3.0 * P, None,
                                          ALU.add).then_inc(prep_step, 1)
                    else:
                        dve.wait_ge(prep_step, j.count(3, 3))
                        dve.tensor_tensor(
                            pen[:, k, 0:HEADS * FRAME].rearrange("p (h f) -> p h f", f=FRAME)[:, :, 2:TILES + 1],
                            dlb[:, k, None, 0:TILES - 1].broadcast_to([P, HEADS, TILES - 1]),
                            dlb[:, k, None, 1:TILES].broadcast_to([P, HEADS, TILES - 1]),
                            ALU.subtract).then_inc(prepped, 1)

                def scans(k):
                    dve.tensor_tensor_scan(fwd[:, :, :].rearrange("p h f -> p (h f)"), pen[:, k, 0:HEADS * FRAME],
                                           frame_flat(logit, k), -BIG, ALU.add, ALU.max)
                    return dve.tensor_tensor_scan(bwd[:, :, :].rearrange("p h f -> p (h f)")[:, ::-1],
                                                  pen[:, k, 1:HEADS * FRAME + 1][:, ::-1],
                                                  frame_flat(logit, k)[:, ::-1], -BIG, ALU.add, ALU.max)

                def slot(i, g):
                    par = g % 2
                    coming, before, third = i.shift(1), i.shift(-1), i.shift(-3)
                    if i.exists:
                        dve.wait_ge(exp_done, i.count(GROUPS, g + 1))
                        dve.tensor_scalar(e_buf[:, par], e_buf[:, par], E_MAX, None, ALU.min).then_inc(cut_done, 1)
                    j, h = behind(i, g, 1)
                    if j.exists:
                        if j.positive(GROUPS, h - 1):
                            dve.wait_ge(score_done, j.count(GROUPS, h - 1))
                        for hf in range(2):
                            dve.wait_ge(r_done, j.count(2 * GROUPS, 2 * h + hf + 1))
                            dve.scalar_tensor_tensor(h_buf[:, 1 - par, hf], e_buf[:, 1 - par, hf], 0.5,
                                                     z_ps[:, 1 - par, hf, 0:COLS], ALU.subtract,
                                                     ALU.mult).then_inc(h_done, 1)
                    if g == 1 and third.exists:
                        dve.wait_ge(yx_done, third.count(1, 1))
                        dve.bn_stats(stats[:, :], yx[:, :]).then_inc(stats_done, 1)
                    if g == 0 and coming.exists:
                        prep(coming, 0)
                    if g == 0 and i.shift(-4).exists:
                        dve.wait_ge(y_free, i.shift(-4).count(1, 1))
                        scale_rows(i.shift(-4).buf, i.shift(-4).count(1))
                    if g == 4 and before.exists:
                        dve.wait_ge(carry_tr, before.count(1, 1))
                        dve.tensor_copy(logit[:, before.buf, :, 0:FRAME:FRAME - 1].rearrange("p h a -> p a h"),
                                        carry_ps.rearrange("p (a h) -> p a h", a=2)).then_inc(carry_in, 1)
                    if before.exists and g == 3:
                        dve.wait_ge(scan_tr, before.count(1, 1))
                        dve.wait_ge(pens_done, before.count(1, 1))
                        dve.tensor_tensor_scan(tf[:, :], penf[:, 0, :], edge_first_ps[:, 0:P], -BIG, ALU.add, ALU.max)
                        dve.tensor_tensor_scan(tb[:, ::-1], penb[:, 0, ::-1], edge_first_ps[:, P:2 * P][:, ::-1], -BIG,
                                               ALU.add, ALU.max).then_inc(tscan_done, 1)
                    j, h = behind(i, g, -5)
                    if j.exists:
                        old = j.shift(-3)
                        dve.wait_ge(prep_step, j.count(3, 1))
                        if old.exists:
                            dve.wait_ge(out_done, old.count(GROUPS, h + 1))
                        dve.tensor_tensor(
                            sel[:, j.buf, GROUP * h:GROUP * (h + 1), :],
                            node_col[:, None, :].broadcast_to([P, GROUP, P]),
                            dl[:, j.buf, GROUP * h:GROUP * (h + 1), None].broadcast_to([P, GROUP, P]),
                            ALU.is_equal).then_inc(sel_done, 1)
                    if g == 1 and coming.exists:
                        prep(coming, 1)
                    if before.exists and g == 2:
                        dve.wait_ge(logit_done, before.count(2, 2))
                        scans(before.buf).then_inc(scan_done, 1)
                    if before.exists and g == 3:
                        dve.wait_ge(tscan_done, before.count(1, 1))
                        dve.tensor_tensor(carry[:, 0, 1:P], tf[:, 0:P - 1], penf[:, 1, 1:P], ALU.add)
                        dve.tensor_tensor(carry[:, 1, 0:P - 1], tb[:, 1:P], penb[:, 1, 0:P - 1],
                                          ALU.add).then_inc(carry_done, 1)
                    if before.exists and g == 4:
                        dve.wait_ge(carry_in, before.count(1, 1))
                        scans(before.buf).then_inc(rescan_done, 1)
                    b = i.shift(-2)
                    if g == GROUPS - 1 and b.exists:
                        dve.wait_ge(out_done, b.count(GROUPS, GROUPS))
                        dve.tensor_scalar(den[:, :], acc_ps[:, D:ROW], 1e-30, None, ALU.max).then_inc(den_done, 1)
                    j, h = behind(i, g, 11)
                    if j.exists:
                        dve.wait_ge(p_done, j.count(1, 1))
                        rows = s_buf[:, j.buf, GROUP * h:GROUP * (h + 1), :]
                        sent = rows[:, :, 0:D].rearrange("p j (h c) -> p j h c", h=HEADS)
                        dve.tensor_tensor(sent, sent, rows[:, :, D:ROW][:, :, :, None].broadcast_to([P, GROUP, HEADS, HD]),
                                          ALU.mult).then_inc(msg_done, 1)
                    if before.exists and g == 4:
                        dve.wait_ge(rescan_done, before.count(1, 1))
                        dve.tensor_tensor(top[:, :, :], fwd[:, :, 1:TILES + 1], bwd[:, :, 1:TILES + 1],
                                          ALU.max).then_inc(top_done, 1)
                    if g == 1 and coming.exists:
                        prep(coming, 2)
                    if g == 0 and third.exists:
                        dve.wait_ge(acc_read, third.count(1, 1))
                        dve.wait_ge(x_in[third.buf], third.uses(16))
                        if third.positive(1):
                            dve.wait_ge(y_done, third.count(1))
                        dve.tensor_tensor(yx[:, :], y[:, :], x_buf[:, third.buf, :], ALU.add).then_inc(yx_done, 1)
                    if g == GROUPS - 1 and b.exists:
                        dve.wait_ge(den_done, b.count(1, 1))
                        dve.reciprocal(rden[:, :], den[:, :]).then_inc(rden_done, 1)
                        dve.wait_ge(rden_done, b.count(1, 1))
                        dve.tensor_tensor(y[:, :].rearrange("p (h c) -> p h c", h=HEADS),
                                          acc_ps[:, 0:D].rearrange("p (h c) -> p h c", h=HEADS),
                                          rden[:, :, None].broadcast_to([P, HEADS, HD]), ALU.mult).then_inc(acc_read, 1)
                    if before.exists and g == 4:
                        dve.wait_ge(top_done, before.count(1, 1))
                        dve.tensor_tensor(diff[:, :, :], logit[:, before.buf, :, 1:TILES + 1], top[:, :, :],
                                          ALU.subtract).then_inc(diff_done, 1)
                    if g == 1 and third.exists:
                        dve.wait_ge(stats_done, third.count(1, 1))
                        dve.sem_inc(dve_passed, 1)
                        dve.bn_aggr(mv[:, :], stats[:, :]).then_inc(mv_done, 1)

                def body(i):
                    for g in range(GROUPS):
                        slot(i, g)

                iterations(dve, body, last=blocks + 4, peeled=2)

            def tiles_path():
                dve.memset(g_old[:, 0:ROW], 0.0)
                dve.memset(g_old[:, ROW:ROW + HEADS], -BIG).then_inc(g_first_made, 1)
                with dve.Fori(0, edge_tiles) as t:
                    def step(n):
                        dve.wait_ge(g_step, t * 11 + n)

                    dve.wait_ge(g_edges, t * 32 + 32)
                    dve.tensor_scalar(g_node[:, :], g_dst[:, :], float(n_nodes - 1), None, ALU.min)
                    dve.tensor_scalar(g_row[:, :], g_dst[:, :], float(blocks * P), None, ALU.min)
                    dve.tensor_scalar(g_dstf[:, :], g_dst[:, :], float(blocks * P), None, ALU.min).then_inc(g_index, 1)
                    dve.wait_ge(g_gathered, t * 48 + 48)
                    dve.tensor_tensor(g_h, g_r[:, 0:D], g_r[:, D:2 * D], ALU.add).then_inc(g_step, 1)
                    step(1)
                    dve.tensor_tensor(g_z, g_h, g_sp[:, 0:D], ALU.add).then_inc(g_z_done, 1)
                    dve.wait_ge(g_dst_all, t + 1)
                    dve.tensor_scalar(g_like[:, :], g_dst_ps, g_dstf[:, 0:1], None, ALU.is_equal).then_inc(g_step, 1)
                    step(2)
                    dve.tensor_scalar(g_pen[:, :], g_like[:, :], -1.0, BIG, ALU.add, ALU.mult).then_inc(g_step, 1)
                    dve.wait_ge(g_e_done, t + 1)
                    dve.tensor_scalar(g_e, g_e, E_MAX, None, ALU.min).then_inc(g_cut_done, 1)
                    dve.wait_ge(g_r_done, t + 1)
                    dve.scalar_tensor_tensor(g_h, g_e, 0.5, g_z, ALU.subtract, ALU.mult).then_inc(g_step, 1)
                    step(4)
                    by_head = g_h.rearrange("p (h c) -> p h c", h=HEADS)
                    dve.tensor_tensor(by_head, by_head, aw_row[:, None, :].broadcast_to([P, HEADS, HD]),
                                      ALU.mult).then_inc(g_step, 1)
                    step(5)
                    dve.reduce_sum(g_logit0[:, :], by_head, mybir.AxisListType.X).then_inc(g_step, 1)
                    step(6)
                    dve.tensor_scalar(g_logit[:, :], g_logit0[:, :], -2.0, ab_sb[:, 0:1], ALU.mult,
                                      ALU.add).then_inc(g_logit_done, 1)
                    dve.wait_ge(g_logit_all, t + 1)
                    step(3)
                    for hf in range(2):
                        last = dve.tensor_tensor(
                            g_masked[:, 4 * hf:4 * hf + 4, :], g_logit_ps[:, hf, :].rearrange("p (h e) -> p h e", e=P),
                            g_pen[:, None, :].broadcast_to([P, 4, P]), ALU.add)
                    last.then_inc(g_step, 1)
                    step(7)
                    dve.reduce_max(g_max[:, :], g_masked, mybir.AxisListType.X).then_inc(g_step, 1)
                    step(8)
                    old_max = g_old[:, ROW:ROW + HEADS]
                    new_max = g_new[:, ROW:ROW + HEADS]
                    dve.tensor_tensor(new_max, g_max[:, :], old_max, ALU.max).then_inc(g_step, 1)
                    step(9)
                    dve.tensor_tensor(g_drop[:, :], old_max, new_max, ALU.subtract).then_inc(g_step, 1)
                    dve.tensor_tensor(g_args[:, 0, :], g_logit[:, :], new_max, ALU.subtract)
                    step(10)
                    dve.tensor_scalar(g_args[:, 1, :], g_drop[:, :], -100.0, None, ALU.max).then_inc(g_args_done, 1)
                    dve.wait_ge(g_p_done, t + 1)
                    sent = g_sp[:, 0:D].rearrange("p (h c) -> p h c", h=HEADS)
                    dve.tensor_tensor(sent, sent, g_sp[:, D:ROW, None].broadcast_to([P, HEADS, HD]),
                                      ALU.mult).then_inc(g_msg_done, 1)
                    dve.tensor_tensor(g_old[:, 0:D].rearrange("p (h c) -> p h c", h=HEADS),
                                      g_old[:, 0:D].rearrange("p (h c) -> p h c", h=HEADS),
                                      g_fade[:, :, None].broadcast_to([P, HEADS, HD]), ALU.mult)
                    dve.tensor_tensor(g_old[:, D:ROW], g_old[:, D:ROW], g_fade[:, :], ALU.mult).then_inc(g_step, 1)
                    step(11)
                    dve.wait_ge(g_sum_done, t + 1)
                    dve.tensor_tensor(g_new[:, 0:ROW], g_old[:, 0:ROW], g_sum_ps, ALU.add).then_inc(g_new_done, 1)

                def finish(b):
                    dve.wait_ge(g_rows_in, b * 32 + 32)
                    dve.tensor_scalar(den[:, :], g_old[:, D:ROW], 1e-30, None, ALU.max).then_inc(den_done, 1)
                    dve.wait_ge(den_done, b + 1)
                    dve.reciprocal(rden[:, :], den[:, :]).then_inc(rden_done, 1)
                    dve.wait_ge(rden_done, b + 1)
                    dve.tensor_tensor(y[:, :].rearrange("p (h c) -> p h c", h=HEADS),
                                      g_old[:, 0:D].rearrange("p (h c) -> p h c", h=HEADS),
                                      rden[:, :, None].broadcast_to([P, HEADS, HD]), ALU.mult).then_inc(acc_read, 1)
                    dve.wait_ge(acc_read, b + 1)
                    dve.tensor_tensor(yx[:, :], y[:, :], x_buf[:, 0, :], ALU.add).then_inc(yx_done, 1)
                    dve.wait_ge(yx_done, b + 1)
                    dve.bn_stats(stats[:, :], yx[:, :]).then_inc(stats_done, 1)
                    dve.wait_ge(stats_done, b + 1)
                    dve.sem_inc(dve_passed, 1)
                    dve.bn_aggr(mv[:, :], stats[:, :]).then_inc(mv_done, 1)
                    scale_rows(0, b)

                with dve.Fori(0, blocks) as b:
                    finish(b)

            dve.wait_ge(s_drops_row, 1)
            dve.reduce_max(unfit[0:1, 0:1], pm[0:1, 3, 0:P], mybir.AxisListType.X)
            dve.wait_ge(s_starts, 16)
            dve.tensor_tensor(runs[:, :], starts[0:1, 1:bounds], starts[0:1, 0:blocks], ALU.subtract).then_inc(s_plan_step, 1)
            dve.wait_ge(s_plan_step, 1)
            dve.reduce_max(unfit[0:1, 1:2], runs[:, :], mybir.AxisListType.X).then_inc(s_plan_step, 1)
            dve.wait_ge(s_plan_step, 2)
            dve.tensor_scalar(unfit[0:1, 2:3], unfit[0:1, 1:2], float(BLOCK_EDGES), None, ALU.is_gt).then_inc(s_plan_step, 1)
            dve.wait_ge(s_plan_step, 3)
            dve.tensor_tensor(unfit[0:1, 3:4], unfit[0:1, 2:3], unfit[0:1, 0:1], ALU.add).then_inc(s_plan_step, 1)
            dve.wait_ge(s_plan_step, 4)
            dve.tensor_scalar(plan[0:1, 0:1], unfit[0:1, 3:4], 1.0, None, ALU.min).then_inc(s_plan, 1)

            dve.wait_ge(s_plan, 1)
            plan_now = dve.value_load(plan[0:1, 0:1], min_val=0, max_val=1)
            with dve.If(plan_now == 0):
                blocks_path()
            with dve.Else():
                tiles_path()


_INS = ['x', 'src', 'dst', 'L0_gnn_Wi', 'L0_gnn_bi', 'L0_gnn_Wj', 'L0_gnn_bj', 'L0_gnn_a_w', 'L0_gnn_a_b']
_SHAPES = {'L0_gnn_Wi': (D, D), 'L0_gnn_bi': (1, D), 'L0_gnn_Wj': (D, D), 'L0_gnn_bj': (1, D),
           'L0_gnn_a_w': (HD, 1), 'L0_gnn_a_b': (1, 1)}


def kernel(**inputs):
    import numpy as _np
    import concourse.bacc as _bacc
    from concourse import mybir as _mybir
    from concourse.bass_utils import run_bass_kernel_spmd as _run

    nc = _bacc.Bacc("TRN2", target_bir_lowering=False, num_devices=1)
    arrays, args = {}, []
    for name in _INS:
        a = _np.ascontiguousarray(inputs[name])
        a = a.reshape(_SHAPES.get(name, a.shape))
        arrays[f"in_{name}_dram"] = a
        args.append(nc.dram_tensor(f"in_{name}_dram", a.shape, _mybir.dt.from_np(a.dtype), kind="ExternalInput").ap())
    shape = arrays["in_x_dram"].shape
    args.append(nc.dram_tensor("out_0_dram", shape, F32, kind="ExternalOutput").ap())
    gnn_program(nc, *args)
    r = _run(nc, [arrays], core_ids=[0])
    return r.results[0]["out_0_dram"]
```
